# Optimizing a Trainium2 kernel written in Bass

```python
import numpy as np
import jax
import jax.numpy as jnp

def _softmax(x, axis=-1):
    return jax.nn.softmax(x, axis=axis)

def _gelu(x):
    return jax.nn.gelu(x, approximate=True)

def _silu(x):
    return jax.nn.silu(x)

def _sigmoid(x):
    return jax.nn.sigmoid(x)

def _layernorm(x, axis=-1, eps=1e-05):
    m = jnp.mean(x, axis=axis, keepdims=True)
    v = jnp.var(x, axis=axis, keepdims=True)
    return (x - m) / jnp.sqrt(v + eps)

def _scatter_add(tgt, idx, src, axis=0):
    return tgt.at[idx].add(src)

def _segment_sum(src, seg, n):
    return jax.ops.segment_sum(src, seg, n)
kernel_name = 'mk_decoder_postln_d2_seqx_r8_d44100'

def setup_inputs(seed: int=0):
    np.random.seed(seed)
    _w = jnp.asarray

    def _rec_inputs():
        import jax
        import jax.numpy as jnp
        _rk = jax.random.key(seed)
        x = -0.0002928 + 1 * jax.random.normal(jax.random.fold_in(_rk, 1), (4, 512, 128), jnp.float32)
        _lenS = 512 - jax.random.randint(jax.random.fold_in(_rk, 7), (4,), 0, max(1, 512 // 4) + 1, jnp.int32)
        _lenS2 = 154 - jax.random.randint(jax.random.fold_in(_rk, 8), (4,), 0, max(1, 154 // 4) + 1, jnp.int32)
        _ctx_1024P = jax.random.normal(jax.random.fold_in(_rk, 11), (4, 16, 128), jnp.float32)
        _ctx_1024c = jax.random.dirichlet(jax.random.fold_in(_rk, 511), 0.3 * jnp.ones((16,), jnp.float32), (4, 154))
        _ctx_1024t = jnp.einsum('bsk,bkd->bsd', _ctx_1024c, _ctx_1024P)
        _ctx_1024t = _ctx_1024t * jax.lax.rsqrt(jnp.mean(jnp.square(_ctx_1024t)) + 1e-12) * 0.953939
        ctx_1024 = -1.39393e-06 + 0.999914 * (_ctx_1024t + 0.3 * jax.random.normal(jax.random.fold_in(_rk, 611), (4, 154, 128), jnp.float32))
        return (x, ctx_1024)
    x, ctx_1024 = _rec_inputs()

    def _L0_attn_setup():
        import jax, jax.numpy as jnp
        import numpy as np
        N_HEAD = 16
        EPS = 1e-06

        def _linear_attention(q, k, v):
            B, H, D = (q.shape[1], q.shape[2], q.shape[3])

            def step(carry, qkv_t):
                S, z = carry
                qt, kt, vt = qkv_t
                S = S + kt[..., :, None] * vt[..., None, :]
                z = z + kt
                num = jnp.einsum('bhi,bhij->bhj', qt, S)
                den = jnp.sum(qt * z, axis=-1, keepdims=True)
                return ((S, z), num / (den + EPS))
            S0 = jnp.zeros((B, H, D, D), q.dtype)
            z0 = jnp.zeros((B, H, D), q.dtype)
            _, y = jax.lax.scan(step, (S0, z0), (q, k, v))
            return y
        key = jax.random.key(seed)
        k1, k2, k3 = jax.random.split(key, 3)
        B, T, C = (2, 256, 128)
        x = jax.random.normal(k1, (B, T, C), dtype=jnp.float32)
        w_attn = jax.random.normal(k2, (C, 3 * C), dtype=jnp.float32) * 0.02
        w_proj = jax.random.normal(k3, (C, C), dtype=jnp.float32) * 0.02
        return {'x': x, 'w_attn': w_attn, 'w_proj': w_proj}
    _L0_attn_all = _L0_attn_setup()
    _L0_attn_in = {k: v for k, v in _L0_attn_all.items() if k in ('w_attn', 'w_proj')}
    del _L0_attn_all

    def _L0_xattn_setup():
        import jax, jax.numpy as jnp
        import numpy as np
        DIM = 128
        NUM_HEADS = 16
        HEAD_DIM = DIM // NUM_HEADS
        key = jax.random.key(seed)
        ks = jax.random.split(key, 11)
        B, N, C = (2, 256, DIM)
        s = 1.0 / np.sqrt(C)
        inp = {'q': jax.random.normal(ks[0], (B, N, C), jnp.float32), 'k': jax.random.normal(ks[1], (B, N, C), jnp.float32), 'v': jax.random.normal(ks[2], (B, N, C), jnp.float32), 'Wq': jax.random.normal(ks[3], (C, C), jnp.float32) * s, 'bq': jnp.zeros((C,), jnp.float32), 'Wk': jax.random.normal(ks[4], (C, C), jnp.float32) * s, 'bk': jnp.zeros((C,), jnp.float32), 'Wv': jax.random.normal(ks[5], (C, C), jnp.float32) * s, 'bv': jnp.zeros((C,), jnp.float32), 'Wo': jax.random.normal(ks[6], (C, C), jnp.float32) * s, 'bo': jnp.zeros((C,), jnp.float32)}
        return inp
    _L0_xattn_all = _L0_xattn_setup()
    _L0_xattn_in = {k: v for k, v in _L0_xattn_all.items() if k in ('Wq', 'bq', 'Wk', 'bk', 'Wv', 'bv', 'Wo', 'bo')}
    del _L0_xattn_all

    def _L0_ffn_setup():
        import jax, jax.numpy as jnp
        import numpy as np
        MAX_VAL = 100.0
        key = jax.random.key(seed)
        k1, k2, k3 = jax.random.split(key, 3)
        B, S, D_IN, D_OUT = (4, 1024, 128, 128)
        x = jax.random.normal(k1, (B, S, D_IN), dtype=jnp.float32)
        weights = jax.random.normal(k2, (D_OUT, D_IN), dtype=jnp.float32)
        scale = jnp.ones((D_OUT,), dtype=jnp.float32)
        bias = jax.random.normal(k3, (D_OUT,), dtype=jnp.float32)
        return {'x': x, 'weights': weights, 'scale': scale, 'bias': bias}
    _L0_ffn_all = _L0_ffn_setup()
    _L0_ffn_in = {k: v for k, v in _L0_ffn_all.items() if k in ('weights', 'scale', 'bias')}
    del _L0_ffn_all

    def _L1_attn_setup():
        import jax, jax.numpy as jnp
        import numpy as np
        D_MODEL = 128
        NUM_HEADS = 16
        D_K = D_MODEL // NUM_HEADS
        SCALE = D_K ** 0.5
        key = jax.random.key(seed)
        k1, k2, k3, k4, k5 = jax.random.split(key, 5)
        B, T = (4, 256)
        x = jax.random.normal(k1, (B, T, D_MODEL), dtype=jnp.float32)
        s = 1.0 / np.sqrt(D_MODEL)
        w_qkv = jax.random.uniform(k2, (D_MODEL, 3 * D_MODEL), jnp.float32, -s, s)
        b_qkv = jax.random.uniform(k3, (3 * D_MODEL,), jnp.float32, -s, s)
        w_out = jax.random.uniform(k4, (D_MODEL, D_MODEL), jnp.float32, -s, s)
        b_out = jax.random.uniform(k5, (D_MODEL,), jnp.float32, -s, s)
        return {'x': x, 'w_qkv': w_qkv, 'b_qkv': b_qkv, 'w_out': w_out, 'b_out': b_out}
    _L1_attn_all = _L1_attn_setup()
    _L1_attn_in = {k: v for k, v in _L1_attn_all.items() if k in ('w_qkv', 'b_qkv', 'w_out', 'b_out')}
    del _L1_attn_all

    def _L1_xattn_setup():
        import jax, jax.numpy as jnp
        import numpy as np
        D_MODEL = 128
        N_HEAD = 16
        D_HEAD = D_MODEL // N_HEAD
        key = jax.random.key(seed)
        ks = jax.random.split(key, 11)
        B, S = (2, 512)
        scale = 1.0 / np.sqrt(D_MODEL)
        inp = {'q': jax.random.normal(ks[0], (B, S, D_MODEL), jnp.float32), 'k': jax.random.normal(ks[1], (B, S, D_MODEL), jnp.float32), 'v': jax.random.normal(ks[2], (B, S, D_MODEL), jnp.float32), 'w_q': jax.random.normal(ks[3], (D_MODEL, D_MODEL), jnp.float32) * scale, 'b_q': jnp.zeros((D_MODEL,), jnp.float32), 'w_k': jax.random.normal(ks[4], (D_MODEL, D_MODEL), jnp.float32) * scale, 'b_k': jnp.zeros((D_MODEL,), jnp.float32), 'w_v': jax.random.normal(ks[5], (D_MODEL, D_MODEL), jnp.float32) * scale, 'b_v': jnp.zeros((D_MODEL,), jnp.float32), 'w_o': jax.random.normal(ks[6], (D_MODEL, D_MODEL), jnp.float32) * scale, 'b_o': jnp.zeros((D_MODEL,), jnp.float32)}
        return inp
    _L1_xattn_all = _L1_xattn_setup()
    _L1_xattn_in = {k: v for k, v in _L1_xattn_all.items() if k in ('w_q', 'b_q', 'w_k', 'b_k', 'w_v', 'b_v', 'w_o', 'b_o')}
    del _L1_xattn_all

    def _L1_ffn_setup():
        import jax, jax.numpy as jnp
        import numpy as np
        B, N, D = (4, 256, 128)
        SPARSITY = 0.01
        key = jax.random.key(seed)
        k1, k2, k3 = jax.random.split(key, 3)
        x = jax.random.normal(k1, (B, N, D), dtype=jnp.float32)
        spatial = jax.random.normal(k2, (D, D), dtype=jnp.float32) * 0.02
        freq = jnp.fft.fft(spatial, axis=-1)
        k = int(D * SPARSITY)
        mag = jnp.abs(freq)
        kth = jax.lax.top_k(mag, k)[0][:, -1:]
        w_sparse = jnp.where(mag >= kth, freq, 0.0 + 0j)
        bias = jax.random.normal(k3, (D,), dtype=jnp.float32) * 0.01
        return {'x': x, 'w_freq_real': jnp.real(w_sparse).astype(jnp.float32), 'w_freq_imag': jnp.imag(w_sparse).astype(jnp.float32), 'bias': bias}
    _L1_ffn_all = _L1_ffn_setup()
    _L1_ffn_in = {k: v for k, v in _L1_ffn_all.items() if k in ('w_freq_real', 'w_freq_imag', 'bias')}
    del _L1_ffn_all
    return {'x': x, 'ctx_1024': ctx_1024, 'L0_attn_w_attn': _L0_attn_in['w_attn'], 'L0_attn_w_proj': _L0_attn_in['w_proj'], 'L0_xattn_Wq': _L0_xattn_in['Wq'], 'L0_xattn_bq': _L0_xattn_in['bq'], 'L0_xattn_Wk': _L0_xattn_in['Wk'], 'L0_xattn_bk': _L0_xattn_in['bk'], 'L0_xattn_Wv': _L0_xattn_in['Wv'], 'L0_xattn_bv': _L0_xattn_in['bv'], 'L0_xattn_Wo': _L0_xattn_in['Wo'], 'L0_xattn_bo': _L0_xattn_in['bo'], 'L0_ffn_weights': _L0_ffn_in['weights'], 'L0_ffn_scale': _L0_ffn_in['scale'], 'L0_ffn_bias': _L0_ffn_in['bias'], 'L1_attn_w_qkv': _L1_attn_in['w_qkv'], 'L1_attn_b_qkv': _L1_attn_in['b_qkv'], 'L1_attn_w_out': _L1_attn_in['w_out'], 'L1_attn_b_out': _L1_attn_in['b_out'], 'L1_xattn_w_q': _L1_xattn_in['w_q'], 'L1_xattn_b_q': _L1_xattn_in['b_q'], 'L1_xattn_w_k': _L1_xattn_in['w_k'], 'L1_xattn_b_k': _L1_xattn_in['b_k'], 'L1_xattn_w_v': _L1_xattn_in['w_v'], 'L1_xattn_b_v': _L1_xattn_in['b_v'], 'L1_xattn_w_o': _L1_xattn_in['w_o'], 'L1_xattn_b_o': _L1_xattn_in['b_o'], 'L1_ffn_w_freq_real': _L1_ffn_in['w_freq_real'], 'L1_ffn_w_freq_imag': _L1_ffn_in['w_freq_imag'], 'L1_ffn_bias': _L1_ffn_in['bias']}

def reference(x, ctx_1024, L0_attn_w_attn, L0_attn_w_proj, L0_xattn_Wq, L0_xattn_bq, L0_xattn_Wk, L0_xattn_bk, L0_xattn_Wv, L0_xattn_bv, L0_xattn_Wo, L0_xattn_bo, L0_ffn_weights, L0_ffn_scale, L0_ffn_bias, L1_attn_w_qkv, L1_attn_b_qkv, L1_attn_w_out, L1_attn_b_out, L1_xattn_w_q, L1_xattn_b_q, L1_xattn_w_k, L1_xattn_b_k, L1_xattn_w_v, L1_xattn_b_v, L1_xattn_w_o, L1_xattn_b_o, L1_ffn_w_freq_real, L1_ffn_w_freq_imag, L1_ffn_bias):
    import jax
    import jax.numpy as jnp

    def _L0_attn_ref(x, w_attn, w_proj):
        import jax, jax.numpy as jnp
        import numpy as np
        N_HEAD = 16
        EPS = 1e-06

        def _linear_attention(q, k, v):
            B, H, D = (q.shape[1], q.shape[2], q.shape[3])

            def step(carry, qkv_t):
                S, z = carry
                qt, kt, vt = qkv_t
                S = S + kt[..., :, None] * vt[..., None, :]
                z = z + kt
                num = jnp.einsum('bhi,bhij->bhj', qt, S)
                den = jnp.sum(qt * z, axis=-1, keepdims=True)
                return ((S, z), num / (den + EPS))
            S0 = jnp.zeros((B, H, D, D), q.dtype)
            z0 = jnp.zeros((B, H, D), q.dtype)
            _, y = jax.lax.scan(step, (S0, z0), (q, k, v))
            return y
        B, T, C = x.shape
        H = N_HEAD
        D = C // H
        qkv = x @ w_attn
        q, k, v = jnp.split(qkv, 3, axis=-1)

        def to_tbhd(a):
            return a.reshape(B, T, H, D).transpose(1, 0, 2, 3)
        q = jax.nn.elu(to_tbhd(q)) + 1.0
        k = jax.nn.elu(to_tbhd(k)) + 1.0
        v = to_tbhd(v)
        y = _linear_attention(q, k, v)
        y = y.transpose(1, 0, 2, 3).reshape(B, T, C)
        return y @ w_proj

    def _L0_xattn_ref(q, k, v, Wq, bq, Wk, bk, Wv, bv, Wo, bo):
        import jax, jax.numpy as jnp
        import numpy as np
        DIM = 128
        NUM_HEADS = 16
        HEAD_DIM = DIM // NUM_HEADS
        B, Nq, C = q.shape
        Nkv = k.shape[1]
        H, D = (NUM_HEADS, HEAD_DIM)
        qh = (q @ Wq.T + bq).reshape(B, Nq, H, D).transpose(0, 2, 1, 3)
        kh = (k @ Wk.T + bk).reshape(B, Nkv, H, D).transpose(0, 2, 1, 3)
        vh = (v @ Wv.T + bv).reshape(B, Nkv, H, D).transpose(0, 2, 1, 3)
        scale = D ** (-0.5)
        attn = jax.nn.softmax(jnp.einsum('bhqd,bhkd->bhqk', qh, kh) * scale, axis=-1)
        out = jnp.einsum('bhqk,bhkd->bhqd', attn, vh)
        out = out.transpose(0, 2, 1, 3).reshape(B, Nq, C)
        return out @ Wo.T + bo

    def _L0_ffn_ref(x, weights, scale, bias):
        import jax, jax.numpy as jnp
        import numpy as np
        MAX_VAL = 100.0
        w = (weights >= 0.0).astype(x.dtype) * 2.0 - 1.0
        y = jnp.einsum('bsi,oi->bso', x, w)
        y = y * scale + bias
        y = jnp.clip(y, -MAX_VAL, MAX_VAL)
        return y

    def _L1_attn_ref(x, w_qkv, b_qkv, w_out, b_out):
        import jax, jax.numpy as jnp
        import numpy as np
        D_MODEL = 128
        NUM_HEADS = 16
        D_K = D_MODEL // NUM_HEADS
        SCALE = D_K ** 0.5
        B, T, D = x.shape
        qkv = x @ w_qkv + b_qkv
        q, k, v = jnp.split(qkv, 3, axis=-1)

        def split_heads(t):
            return t.reshape(B, T, NUM_HEADS, D_K).transpose(0, 2, 1, 3)
        q, k, v = (split_heads(q), split_heads(k), split_heads(v))
        scores = jnp.einsum('bhtd,bhsd->bhts', q, k) / SCALE
        attn = jax.nn.softmax(scores, axis=-1)
        ctx = jnp.einsum('bhts,bhsd->bhtd', attn, v)
        ctx = ctx.transpose(0, 2, 1, 3).reshape(B, T, D)
        y = ctx @ w_out + b_out
        return y

    def _L1_xattn_ref(q, k, v, w_q, b_q, w_k, b_k, w_v, b_v, w_o, b_o):
        import jax, jax.numpy as jnp
        import numpy as np
        D_MODEL = 128
        N_HEAD = 16
        D_HEAD = D_MODEL // N_HEAD
        B, S, _ = q.shape

        def proj(x, w, b):
            y = x @ w.T + b
            return y.reshape(B, -1, N_HEAD, D_HEAD).transpose(0, 2, 1, 3)
        query = proj(q, w_q, b_q)
        key_ = proj(k, w_k, b_k)
        value = proj(v, w_v, b_v)
        scores = jnp.einsum('bhsd,bhtd->bhst', query, key_) / jnp.sqrt(jnp.asarray(D_HEAD, query.dtype))
        attn = jax.nn.softmax(scores, axis=-1)
        out = jnp.einsum('bhst,bhtd->bhsd', attn, value)
        out = out.transpose(0, 2, 1, 3).reshape(B, S, D_MODEL)
        return out @ w_o.T + b_o

    def _L1_ffn_ref(x, w_freq_real, w_freq_imag, bias):
        import jax, jax.numpy as jnp
        import numpy as np
        B, N, D = (4, 256, 128)
        SPARSITY = 0.01
        w = jax.lax.complex(w_freq_real, w_freq_imag)
        x_freq = jnp.fft.fft(x, axis=-1)
        y_freq = jnp.einsum('bnd,do->bno', x_freq, w)
        y = jnp.real(jnp.fft.ifft(y_freq, axis=-1))
        return y + bias
    x = _layernorm(x + _L0_attn_ref(x, L0_attn_w_attn, L0_attn_w_proj), axis=-1)
    x = _layernorm(x + _L0_xattn_ref(x, ctx_1024, ctx_1024, L0_xattn_Wq, L0_xattn_bq, L0_xattn_Wk, L0_xattn_bk, L0_xattn_Wv, L0_xattn_bv, L0_xattn_Wo, L0_xattn_bo), axis=-1)
    x = _layernorm(x + _L0_ffn_ref(x, L0_ffn_weights, L0_ffn_scale, L0_ffn_bias), axis=-1)
    x = _layernorm(x + _L1_attn_ref(x, L1_attn_w_qkv, L1_attn_b_qkv, L1_attn_w_out, L1_attn_b_out), axis=-1)
    x = _layernorm(x + _L1_xattn_ref(x, ctx_1024, ctx_1024, L1_xattn_w_q, L1_xattn_b_q, L1_xattn_w_k, L1_xattn_b_k, L1_xattn_w_v, L1_xattn_b_v, L1_xattn_w_o, L1_xattn_b_o), axis=-1)
    x = _layernorm(x + _L1_ffn_ref(x, L1_ffn_w_freq_real, L1_ffn_w_freq_imag, L1_ffn_bias), axis=-1)
    return x

_drawn_inputs = setup_inputs


def setup_inputs(seed=0):
    import zlib

    import numpy as np

    out = dict(_drawn_inputs(seed))
    spreads = {'L0_xattn_bq': (0.0, 0.38),
     'L0_xattn_bk': (0.0, 0.8),
     'L0_xattn_bv': (0.0, 0.1),
     'L0_xattn_bo': (0.0, 0.1),
     'L0_ffn_scale': (1.0, 0.2),
     'L1_xattn_b_q': (0.0, 0.417),
     'L1_xattn_b_k': (0.0, 0.8),
     'L1_xattn_b_v': (0.0, 0.1),
     'L1_xattn_b_o': (0.0, 0.1)}
    factors = {'L0_attn_w_attn': 8.0, 'L0_attn_w_proj': 8.0, 'L1_ffn_bias': 6.267}
    for name, (base, spread) in spreads.items():
        noise = np.random.default_rng([zlib.crc32(name.encode()), seed]).standard_normal(out[name].shape)
        drawn = base * np.exp(spread * noise) if base else spread * noise
        out[name] = jnp.asarray(drawn.astype(out[name].dtype))
    for name, factor in factors.items():
        out[name] = (out[name] * factor).astype(out[name].dtype)
    return out
```

```python
from contextlib import ExitStack

import numpy as np

import concourse.bass as bass
from concourse import mybir

F32 = mybir.dt.float32
F32R = mybir.dt.float32r
ACT = mybir.ActivationFunctionType
ALU = mybir.AluOpType
AX = mybir.AxisListType

P = 128
B, T, D = 4, 512, 128
S = 154
H, DH = 16, 8
G, J = 4, 4
TT = T // P
SPLIT = 32
ROWS = 3 * SPLIT
VW = 32
TAIL = 32
TAIL_AT = S - TAIL
NS = 2
PAIRS = B // NS
SCALE = float(DH) ** -0.5
EPS_LN = 1e-5
EPS_DEN = 1e-6
MAX_VAL = 100.0

LIN, X0, FFN0, SELF, X1, FFN1 = range(6)
ATTN = (LIN, X0, SELF, X1)


def constants():
    r = np.arange(P)
    k = 2 * np.pi * ((r[:, None] * r[None, :]) % D) / D
    parts = {
        "ident": np.eye(P),
        "cos": np.cos(k),
        "sin": np.sin(k),
        "nsin": -np.sin(k),
        "causal": (r[:, None] <= r[None, :]),
        "headmask": (r[:, None] % SPLIT // DH == np.arange(J)[None, :]),
        "augmask": (r[:, None] >= ROWS) & (r[:, None] < ROWS + 2 * J) & (r[:, None] % J == np.arange(J)[None, :]),
        "tailmask": (r[:, None] % TAIL >= P - TAIL_AT),
        "blockdiag": (r[:, None] // DH == np.arange(H * VW)[None, :] // VW),
    }
    at, out = {}, []
    n = 0
    for name, a in parts.items():
        at[name] = (n, n + a.shape[1])
        n += a.shape[1]
        out.append(a.astype(np.float32))
    return at, np.ascontiguousarray(np.concatenate(out, axis=1))


CONST_AT, CONST = constants()


def attention_steps(s, layer):
    if layer == LIN:
        out = []
        units = [(g, p) for g in range(G) for p in range(2)]
        for n, (g, p) in enumerate(units):
            out.append(("lin_scores", s, layer, g, p))
            if n:
                out.append(("lin_values", s, layer, *units[n - 1]))
        out.append(("lin_values", s, layer, *units[-1]))
        return [], out
    ahead = TT + 1
    maxima = []
    for g in range(G):
        for qt in range(TT):
            parts = [("max", s, layer, g, qt, j) for j in range(J if layer == SELF else 2)]
            if qt == TT - 1:
                parts.append(("shift", s, layer, g))
            maxima.append(parts)
    first = [x for parts in maxima[:ahead] for x in parts]
    later = maxima[ahead:]
    out = []
    if layer == SELF:
        units = [(g, kt) for g in range(G) for kt in range(TT)]
        for n, (g, kt) in enumerate(units):
            m = list(later.pop(0)) if later else []
            out.append(("scores", s, layer, g, kt, 0))
            out += m[0:1]
            out.append(("scores", s, layer, g, kt, 1))
            out += m[1:2]
            if n:
                out.append(("values", s, layer, *units[n - 1]))
            out += m[2:]
        out.append(("values", s, layer, *units[-1]))
    else:
        for g in range(G):
            for part in range(3):
                out.append(("xscores", s, layer, g, part))
                m = later.pop(0) if later else []
                out += m
                if part == 0 and g:
                    out.append(("xvalues", s, layer, g - 1))
            m = later.pop(0) if later else []
            out += m
        out.append(("xvalues", s, layer, G - 1))
    return first, out


def before(s, layer):
    if layer == LIN:
        return [("xt", s, LIN), ("q", s, LIN), ("k", s, LIN), ("v", s, LIN), ("ktok", s, LIN)] + \
               [("state", s, LIN, c) for c in range(TT - 1)]
    if layer == SELF:
        return [("xt", s, SELF), ("q", s, SELF), ("k", s, SELF), ("v", s, SELF)]
    return [("xt", s, layer), ("q", s, layer), ("kx", s, layer), ("vx", s, layer)]


def after(s, layer):
    return [("norm", s, layer, tt) for tt in range(TT)] + [("turn", s, layer), ("y", s, layer)]


def ffn(s, layer):
    return [("xt", s, layer), ("y", s, layer)]


def interleave(main, fill, start=0.0, end=1.0):
    out, done = [], 0
    for n, step in enumerate(main):
        out.append(step)
        f = ((n + 1) / len(main) - start) / (end - start)
        while done < len(fill) and done < f * len(fill):
            out.append(fill[done])
            done += 1
    return out + fill[done:]


def plan():
    steps = [("load", s) for s in range(NS)]
    steps += before(0, LIN)
    fills = before(1, LIN)
    order = [(s, layer) for layer in ATTN for s in range(NS)]
    chains = {LIN: lambda s: after(s, LIN) + before(s, X0),
              X0: lambda s: after(s, X0) + ffn(s, FFN0) + before(s, SELF),
              SELF: lambda s: after(s, SELF) + before(s, X1),
              X1: lambda s: after(s, X1) + ffn(s, FFN1) + [("store", s)]}
    for s, layer in order:
        head, body = attention_steps(s, layer)
        steps += head
        steps += interleave(body, fills)
        fills = chains[layer](s)
    return steps + fills


STEPS = plan()


BIAS_AFTER = {LIN: X0, FFN0: SELF, SELF: X1, X1: FFN1}


def signals(step):
    kind, rest = step[0], step[1:]
    s = rest[0]
    if kind in ("xt", "v", "turn", "norm", "state", "vx"):
        return [("misc_full", step), ("misc_free", step)]
    if kind in ("q", "k", "ktok"):
        out = [("misc_full", step), ("misc_free", step)]
        if rest[1] == LIN:
            out += [("clipped", step), ("exped", step)]
        if kind != "ktok":
            out += [("hi", step)]
            if rest[1] == LIN:
                out += [("lo", step)]
        return out
    if kind == "kx":
        return [("misc_full", step), ("misc_free", step), ("hi", step), ("tail", step)]
    if kind == "max":
        return [("max_full", step), ("max_free", step)]
    if kind == "shift":
        return [("shift_split", step), ("misc_full", step), ("misc_free", step)]
    if kind in ("scores", "xscores"):
        return [("scores_full", step), ("probs", step)]
    if kind == "lin_scores":
        return [("scores_full", step), ("masked", step)]
    if kind in ("values", "lin_values", "xvalues"):
        out = [("values_done", step)]
        if kind == "xvalues" or (kind == "values" and rest[3] == TT - 1) or (kind == "lin_values" and rest[3] == 1):
            out.append(("heads_out", step))
        return out
    if kind == "y":
        out = [("misc_full", step), ("misc_free", step), (f"var{s}", step), (f"rstd{s}", step), (f"x{s}", step)]
        if rest[1] in BIAS_AFTER:
            out.append((f"xb{s}", step))
        return out
    return []


def count():
    value, total = {}, {}
    for step in STEPS:
        for name, key in signals(step):
            total[name] = total.get(name, 0) + 1
            value[name, key] = total[name]
    return value, total


VALUE, TOTAL = count()


def ring(kinds, size):
    place, last, n, held = {}, {}, 0, [None] * size
    for step in STEPS:
        if step[0] in kinds:
            place[step] = n % size
            last[step] = held[n % size]
            held[n % size] = step
            n += 1
    return place, last, held


SCORE_PLACE, SCORE_LAST, SCORE_HELD = ring(("scores", "xscores", "lin_scores"), 2)
MAX_PLACE, MAX_LAST, MAX_HELD = ring(("max",), 2)
MISC = [x for x in STEPS if any(name == "misc_full" for name, _ in signals(x))]
MISC_LAST = {b: a for a, b in zip(MISC, MISC[1:])}
VALUES_KINDS = ("values", "lin_values", "xvalues")
UNITS = [x for x in STEPS if x[0] in VALUES_KINDS]
UNIT_AT = {x: n for n, x in enumerate(UNITS)}
HEADS_OUT = [x for x in UNITS if ("heads_out", x) in signals(x)]
HEADS_LAST = {b: a for a, b in zip(HEADS_OUT, HEADS_OUT[1:])}
PRIMED = ("misc_free", "probs", "masked", "max_free", "heads_out", "x0", "x1")
K_STEPS = [[x for x in STEPS if x[0] in ("k", "kx") and x[1] == s] for s in range(NS)]
K_LAST = {b: a for steps in K_STEPS for a, b in zip(steps, steps[1:])}


def group_end(unit):
    kind, s, layer, g = unit[:4]
    return next(x for x in HEADS_OUT if x[:4] == (kind, s, layer, g))


def chain_length():
    n = 0
    for step in STEPS:
        if step[0] == "shift":
            n += 1
        if step[0] == "norm":
            n += 2 if step[2] == LIN else 1
        if step[0] == "y":
            n += 4 if step[2] == FFN0 else 2
    return n


DVE_CHAIN = chain_length()


def build(nc, x, ctxT, w_lin, w_lin_proj, wx0, bx0, bx0_row, w_ffn0, ffn0_row, w_self, b_self, b_self_row, w_self_out,
          wx1, bx1, bx1_row, w_freq, ffn1_row, const, out):
    with ExitStack() as ctx:
        def sb(name, shape, dt=F32):
            return ctx.enter_context(nc.sbuf_tensor(name, shape, dt))

        def sem(name):
            return ctx.enter_context(nc.semaphore(name))

        C = sb("C", [P, CONST.shape[1]])
        table = {name: C[:, a:b] for name, (a, b) in CONST_AT.items()}
        ident = table["ident"]
        WL = sb("WL", [P, 3 * D])
        WLP = sb("WLP", [P, D])
        WX = [sb(f"WX{i}", [P, 4, D]) for i in range(2)]
        BX = [sb(f"BX{i}", [P, 2]) for i in range(2)]
        BXR = [sb(f"BXR{i}", [P, 2, D]) for i in range(2)]
        WS = sb("WS", [P, 3 * D])
        BS = sb("BS", [P, 2])
        BSR = sb("BSR", [P, 2, D])
        WSO = sb("WSO", [P, D])
        WF0 = sb("WF0", [P, D])
        F0R = sb("F0R", [P, 2, D])
        WFR = sb("WFR", [P, 2, D])
        F1R = sb("F1R", [P, D])
        WF1 = sb("WF1", [P, D])
        GT = sb("GT", [P, 2, D])
        zeros = sb("zeros", [P, T])
        halves = sb("halves", [P, TT])

        def each(name, shape, dt=F32):
            return [sb(f"{name}{s}", shape, dt) for s in range(NS)]

        X = each("X", [P, TT, D])
        XB = each("XB", [P, TT, D])
        XT = each("XT", [P, T])
        CT = each("CT", [P, S])
        SM = each("SM", [P, TT - 1, H * VW])
        QS = each("QS", [P, G, T], F32R)
        KM = each("KM", [P, G, J, T], F32R)
        KT = each("KT", [P, G, J * TAIL], F32R)
        VA = each("VA", [P, TT, H * VW])
        VT = each("VT", [P, G, J * VW])
        OT = each("OT", [P, G, T])
        OC = each("OC", [P, T])
        NEG = each("NEG", [P, TT, J])
        NMP = each("NMP", [P, TT, P])
        O = each("O", [P, TT, D])
        Z = each("Z", [P, TT, D])
        ST6 = each("ST6", [P, TT, 6])
        MV = each("MV", [P, TT, 2])
        VE = each("VE", [P, TT])
        RST = each("RST", [P, TT])
        REC = each("REC", [P, H])
        QF = [OC[s][:, :] for s in range(NS)]
        KF = [OT[s][:, 0, :] for s in range(NS)]
        KTOK = [OT[s][:, 1, :].rearrange("p (t d) -> p t d", t=TT) for s in range(NS)]
        T1 = [OT[s][:, 2, :] for s in range(NS)]
        T2 = [OT[s][:, 3, :] for s in range(NS)]
        HI = [SM[s][:, 0, :].bitcast(F32R) for s in range(NS)]
        LO = [SM[s][:, 1, :].bitcast(F32R) for s in range(NS)]
        KHI = [Z[s][:, :, :].rearrange("p t d -> p (t d)").bitcast(F32R) for s in range(NS)]
        KLO = [O[s][:, :, :].rearrange("p t d -> p (t d)").bitcast(F32R) for s in range(NS)]
        MARK = sb("MARK", [P, 1])
        PR = sb("PR", [P, 2, J, T])
        PT = sb("PT", [P, 2, T])
        BVM = sb("BVM", [P, 2, D])

        SC = [ctx.enter_context(nc.psum_tensor(f"SC{i}", [P, 2, T], F32)) for i in range(2)]
        MX = [ctx.enter_context(nc.psum_tensor(f"MX{i}", [P, T], F32)) for i in range(2)]
        OTP = ctx.enter_context(nc.psum_tensor("OTP", [P, T], F32))
        MISCP = ctx.enter_context(nc.psum_tensor("MISCP", [P, T], F32))

        KD = [nc.dram_tensor(f"KD{s}", (2, P, T), F32, kind="Internal").ap() for s in range(NS)]

        sems = {name: sem(name) for name in TOTAL}
        weights_in = sem("weights_in")
        prep_gpsimd = sem("prep_gpsimd")
        prep_vector = sem("prep_vector")
        prep_tensor = sem("prep_tensor")
        x_in = [sem(f"x_in{s}") for s in range(NS)]
        q_in = [sem(f"q_in{s}") for s in range(NS)]
        k_out = [sem(f"k_out{s}") for s in range(NS)]
        k_in = [sem(f"k_in{s}") for s in range(NS)]
        stored = [sem(f"stored{s}") for s in range(NS)]
        dve_self = sem("dve_self")
        aug_in = sem("aug_in")

        def done(eng, it, name, key):
            eng.wait_ge(sems[name], it * TOTAL[name] + VALUE[name, key] + (name in PRIMED))

        def earlier(eng, it, name):
            assert name in PRIMED
            eng.wait_ge(sems[name], it * TOTAL[name] + 1)

        def misc_empty(eng, it, step):
            if step in MISC_LAST:
                done(eng, it, "misc_free", MISC_LAST[step])
            else:
                earlier(eng, it, "misc_free")

        def score_empty(eng, it, step):
            last = SCORE_LAST[step]
            if last is None:
                earlier(eng, it, "probs")
                earlier(eng, it, "masked")
            else:
                done(eng, it, "masked" if last[0] == "lin_scores" else "probs", last)

        def heads_out_free(eng, it, unit):
            end = group_end(unit)
            if end in HEADS_LAST:
                done(eng, it, "heads_out", HEADS_LAST[end])
            else:
                earlier(eng, it, "heads_out")

        def x_key(s, layer):
            return ("y", s, layer - 1)

        def w_q(layer):
            return {LIN: WL[:, 0:D], SELF: WS[:, 0:D], X0: WX[0][:, 0, :], X1: WX[1][:, 0, :]}[layer]

        def w_k(layer):
            return {LIN: WL[:, D:2 * D], SELF: WS[:, D:2 * D], X0: WX[0][:, 1, :], X1: WX[1][:, 1, :]}[layer]

        def w_v(layer):
            return {LIN: WL[:, 2 * D:], SELF: WS[:, 2 * D:], X0: WX[0][:, 2, :], X1: WX[1][:, 2, :]}[layer]

        def w_out(layer):
            return {LIN: WLP[:, :], SELF: WSO[:, :], X0: WX[0][:, 3, :], X1: WX[1][:, 3, :],
                    FFN0: WF0[:, :], FFN1: WF1[:, :]}[layer]

        def qk_bias(layer, which):
            return {SELF: BS, X0: BX[0], X1: BX[1]}[layer][:, which:which + 1]

        def v_bias(layer):
            return {SELF: BSR, X0: BXR[0], X1: BXR[1]}[layer][:, 0, :]

        def out_bias(layer):
            return {SELF: BSR[:, 1, :], X0: BXR[0][:, 1, :], X1: BXR[1][:, 1, :], FFN1: F1R[:, :]}[layer]

        def spread(row, n):
            return bass.AP(tensor=row.tensor, offset=row.offset, ap=[list(row.ap[0]), [0, n], list(row.ap[-1])])

        LOADS = {}
        loads_total = {}
        for step in STEPS:
            if step[0] in ("q", "k", "kx"):
                name = ("q" if step[0] == "q" else "k", step[1])
                loads_total[name] = loads_total.get(name, 0) + 1
                LOADS[step] = loads_total[name]

        def landed(eng, it, step):
            name = ("q" if step[0] == "q" else "k", step[1])
            s = step[1]
            eng.wait_ge(q_in[s] if step[0] == "q" else k_in[s],
                        (it * loads_total[name] + LOADS[step]) * 16 * 3 * G)

        NW = 17
        N_GPREP = 2 + NS * 4 + 1
        N_VPREP = 4 + 2 + J * (1 + 2 * NS)
        block = ctx.enter_context(nc.Block())

        @block.sync
        def _(sp):
            row = lambda r: bass.AP(tensor=r.tensor, offset=r.offset, ap=[[0, P]] + [list(a) for a in r.ap])
            for dst, src in ((C[:, :], const), (WL[:, :], w_lin), (WLP[:, :], w_lin_proj),
                             (WX[0][:, :, :], wx0), (WX[1][:, :, :], wx1), (BX[0][:, :], bx0), (BX[1][:, :], bx1),
                             (BXR[0][:, :, :], row(bx0_row)), (BXR[1][:, :, :], row(bx1_row)),
                             (WS[:, :], w_self), (BS[:, :], b_self), (BSR[:, :, :], row(b_self_row)),
                             (WSO[:, :], w_self_out), (WF0[:, :], w_ffn0), (F0R[:, :, :], row(ffn0_row)),
                             (WFR[:, :, :], w_freq), (F1R[:, :], row(ffn1_row))):
                sp.dma_start(dst, src).then_inc(weights_in, 16)
            sp.wait_ge(prep_vector, N_VPREP)
            for s in range(NS):
                for g in range(G):
                    sp.dma_start(KM[s][ROWS:P, g, :, :].bitcast(F32), PR[ROWS:P, 0, :, :]).then_inc(aug_in, 16)
            sp.wait_ge(prep_gpsimd, N_GPREP)
            with sp.Fori(0, PAIRS) as it:
                for step in STEPS:
                    kind, s = step[0], step[1]
                    if kind in ("q", "k", "kx"):
                        done(sp, it, "lo" if step[2] == LIN else "misc_free", step)
                        if kind == "q":
                            for blk, part in enumerate((HI[s], HI[s], LO[s])):
                                for g in range(G):
                                    sp.dma_start(QS[s][SPLIT * blk:SPLIT * blk + SPLIT, g, :].bitcast(F32),
                                                 part[SPLIT * g:SPLIT * g + SPLIT, :].bitcast(F32))\
                                      .then_inc(q_in[s], 16)
                            continue
                        n = S if kind == "kx" else T
                        sp.dma_start(KD[s][0, :, 0:n], KHI[s][:, 0:n].bitcast(F32)).then_inc(k_out[s], 16)
                        sp.dma_start(KD[s][1, :, 0:n], KLO[s][:, 0:n].bitcast(F32)).then_inc(k_out[s], 16)
                        sp.wait_ge(k_out[s], (it * loads_total["k", s] + LOADS[step]) * 32)
                        for j in range(J):
                            for blk, part in enumerate((0, 1, 0)):
                                r = SPLIT * blk + DH * j
                                src = KD[s][part].rearrange("(g j d) t -> j d g t", g=G, j=J)[j, :, :, 0:n]
                                sp.dma_start(KM[s][r:r + DH, :, j, 0:n].bitcast(F32), src).then_inc(k_in[s], 16)

        @block.gpsimd
        def _(pool):
            n0 = 0
            for ap, v in [(zeros[:, :], 0.0), (halves[:, :], -0.5)]:
                nc.gpsimd.memset(ap, v).then_inc(prep_gpsimd, 1)
                n0 += 1
            for s in range(NS):
                for ap in (KM[s][0:ROWS, :, :, :].bitcast(F32), VA[s][:, :, :], NMP[s][:, :, :], VT[s][:, :, :]):
                    nc.gpsimd.memset(ap, 0.0).then_inc(prep_gpsimd, 1)
                    n0 += 1
            pool.wait_ge(prep_gpsimd, n0)
            pool.wait_ge(weights_in, 16 * NW)
            last = None
            for s in range(NS):
                for tt in range(TT):
                    v = VA[s][:, tt, :].rearrange("p (h c) -> p h c", c=VW)
                    last = nc.gpsimd.memset(v[:, :, DH:DH + 1], 1.0)
            last.then_inc(prep_gpsimd, 1)
            with pool.Fori(0, PAIRS) as it:
                for step in STEPS:
                    kind, s = step[0], step[1]
                    if kind == "kx":
                        landed(pool, it, step)
                        nc.gpsimd.tensor_tensor(KT[s][0:ROWS, :, :].rearrange("p g (j n) -> p (g j) n", j=J),
                                                KM[s][0:ROWS, :, :, TAIL_AT:S].rearrange("p g j n -> p (g j) n")
                                                .bitcast(F32),
                                                zeros[0:ROWS, :].rearrange("p (a n) -> p a n", n=TAIL), ALU.add)\
                          .then_inc(sems["tail"], 1)
                    if kind == "y":
                        layer = step[2]
                        done(pool, it, f"var{s}", step)
                        nc.gpsimd.tensor_tensor(RST[s][:, :], VE[s][:, :], halves[:, :], ALU.pow)\
                          .then_inc(sems[f"rstd{s}"], 1)
                        if layer in BIAS_AFTER:
                            done(pool, it, f"x{s}", step)
                        if layer in BIAS_AFTER:
                            nc.gpsimd.tensor_tensor(XB[s][:, :, :], X[s][:, :, :],
                                                    spread(out_bias(BIAS_AFTER[layer]), TT), ALU.add)\
                              .then_inc(sems[f"xb{s}"], 1)

        @block.scalar
        def _(act):
            for name in ("probs", "heads_out"):
                act.sem_inc(sems[name], 1)
            for s in range(NS):
                act.sem_inc(stored[s], 1)
            act.wait_ge(weights_in, 16 * NW)
            with act.Fori(0, PAIRS) as it:
                for step in STEPS:
                    kind, s = step[0], step[1]
                    if kind == "load":
                        earlier(act, it, f"x{s}")
                        act.wait_ge(stored[s], it * 16 + 1)
                        act.dma_start(X[s][:, :, :], x[bass.ds(it * NS + s, 1), :, :].rearrange(
                            "b (t p) d -> p (b t) d", p=P)).then_inc(x_in[s], 16)
                        act.dma_start(CT[s][:, :], ctxT[bass.ds(it * NS + s, 1), :, :].rearrange(
                            "b p n -> p (b n)")).then_inc(x_in[s], 16)
                    if kind == "store":
                        done(act, it, f"x{s}", ("y", s, FFN1))
                        act.dma_start(out[bass.ds(it * NS + s, 1), :, :].rearrange("b (t p) d -> p (b t) d", p=P),
                                     X[s][:, :, :]).then_inc(stored[s], 16)
                    if kind == "xt":
                        done(act, it, "misc_full", step)
                        nc.scalar.activation(XT[s][:, :], MISCP[:, :], ACT.Copy).then_inc(sems["misc_free"], 1)
                    if kind == "turn":
                        done(act, it, "misc_full", step)
                        nc.scalar.activation(OC[s][:, :], MISCP[:, :], ACT.Copy).then_inc(sems["misc_free"], 1)
                    if kind in ("q", "k", "ktok") and step[2] == LIN:
                        done(act, it, "clipped", step)
                        nc.scalar.activation(T2[s], T1[s], ACT.Exp).then_inc(sems["exped"], 1)
                        if kind != "ktok":
                            done(act, it, "misc_free", step)
                            nc.scalar.activation((HI if kind == "q" else KHI)[s][:, :],
                                                 (QF if kind == "q" else KF)[s], ACT.Copy)\
                              .then_inc(sems["hi"], 1)
                    elif kind in ("q", "k", "kx"):
                        n = S if kind == "kx" else T
                        done(act, it, "misc_full", step)
                        if step in K_LAST:
                            landed(act, it, K_LAST[step])
                        nc.scalar.activation((HI if kind == "q" else KHI)[s][:, 0:n], MISCP[:, 0:n], ACT.Identity,
                                             bias=qk_bias(step[2], 0 if kind == "q" else 1)).then_inc(sems["hi"], 1)
                    if kind == "shift":
                        done(act, it, "misc_full", step)
                        nc.scalar.activation(QS[s][ROWS:P, step[3], :], MISCP[ROWS:P, :], ACT.Copy)\
                          .then_inc(sems["misc_free"], 1)
                    if kind == "scores":
                        _, _, layer, g, kt, half = step
                        place = SCORE_PLACE[step]
                        unit = UNIT_AT[("values", s, layer, g, kt)]
                        done(act, it, "scores_full", step)
                        if unit >= 2:
                            done(act, it, "values_done", UNITS[unit - 2])
                        nc.scalar.activation(PR[:, unit % 2, 2 * half:2 * half + 2, :], SC[place][:, :, :], ACT.Exp,
                                             scale=SCALE).then_inc(sems["probs"], 1)
                    if kind == "xscores":
                        _, _, layer, g, part = step
                        place = SCORE_PLACE[step]
                        unit = UNIT_AT[("xvalues", s, layer, g)]
                        done(act, it, "scores_full", step)
                        if unit >= 2:
                            done(act, it, "values_done", UNITS[unit - 2])
                        if part < 2:
                            nc.scalar.activation(PR[:, unit % 2, 2 * part:2 * part + 2, :], SC[place][:, :, :],
                                                 ACT.Exp, scale=SCALE).then_inc(sems["probs"], 1)
                        else:
                            nc.scalar.activation(PT[:, unit % 2, :], SC[place][:, 0, :], ACT.Exp,
                                                 scale=SCALE).then_inc(sems["probs"], 1)
                    if ("heads_out", step) in signals(step):
                        done(act, it, "values_done", step)
                        nc.scalar.activation(OT[s][:, step[3], :], OTP[:, :], ACT.Copy).then_inc(sems["heads_out"], 1)
            for s in range(NS):
                act.wait_ge(stored[s], PAIRS * 16 + 1)

        @block.vector
        def _(dve):
            for name in ("misc_free", "masked", "max_free", "x0", "x1"):
                dve.sem_inc(sems[name], 1)
            dve.wait_ge(weights_in, 16 * NW)
            nc.vector.tensor_scalar(GT[:, 0, :], WF0[:, :], 0.0, 2.0, ALU.is_ge, ALU.mult).then_inc(prep_vector, 1)
            dve.wait_ge(prep_vector, 1)
            nc.vector.scalar_tensor_tensor(WF0[:, :], GT[:, 0, :], -1.0, F0R[:, 0, :], ALU.add, ALU.mult)\
              .then_inc(prep_vector, 1)
            dve.wait_ge(prep_vector, 2)
            dve.wait_ge(prep_tensor, 1)
            nc.vector.tensor_copy(GT[:, :, :], MISCP[:, 0:2 * D].rearrange("p (a d) -> p a d", a=2))\
              .then_inc(prep_vector, 1)
            dve.wait_ge(prep_tensor, 2)
            nc.vector.tensor_scalar(WF1[:, :], MISCP[:, 0:D], 1.0 / D, None, ALU.mult).then_inc(prep_vector, 1)
            for i in range(2):
                nc.vector.tensor_scalar(BVM[:, i, :], BXR[i][:, 0, :], table["tailmask"], None, ALU.mult)\
                  .then_inc(prep_vector, 1)
            dve.wait_ge(prep_gpsimd, N_GPREP)
            for j in range(J):
                aug = table["augmask"][ROWS:P, j:j + 1]
                nc.vector.tensor_scalar(PR[ROWS:P, 0, j, :], zeros[ROWS:P, :], aug, None, ALU.add)\
                  .then_inc(prep_vector, 1)
                for s in range(NS):
                    nc.vector.tensor_scalar(KT[s][ROWS:P, :, j * TAIL:j * TAIL + TAIL],
                                            zeros[ROWS:P, 0:G * TAIL].rearrange("p (g n) -> p g n", g=G), aug, None,
                                            ALU.add).then_inc(prep_vector, 1)
                    r = slice(VW * j, VW * j + VW)
                    nc.vector.tensor_scalar(VT[s][r, :, VW * j + DH], zeros[r, 0:G], table["tailmask"][r, :], None,
                                            ALU.add).then_inc(prep_vector, 1)
            dve.wait_ge(prep_vector, N_VPREP)
            dve.wait_ge(aug_in, 16 * NS * G)
            with dve.Fori(0, PAIRS) as it:
                chain = [0]
                CH = DVE_CHAIN

                def link(ins):
                    chain[0] += 1
                    ins.then_inc(dve_self, 1)
                    dve.wait_ge(dve_self, it * CH + chain[0])

                for step in STEPS:
                    kind, s = step[0], step[1]
                    if kind in ("q", "k", "ktok") and step[2] == LIN:
                        done(dve, it, "misc_full", step)
                        nc.vector.tensor_scalar(T1[s], MISCP[:, :], 0.0, None, ALU.min).then_inc(sems["clipped"], 1)
                        done(dve, it, "exped", step)
                        dst = {"q": QF[s], "k": KF[s], "ktok": OT[s][:, 1, :]}[kind]
                        nc.vector.scalar_tensor_tensor(dst, MISCP[:, :], 0.0, T2[s], ALU.max, ALU.add)\
                          .then_inc(sems["misc_free"], 1)
                        if kind != "ktok":
                            done(dve, it, "hi", step)
                            done(dve, it, "misc_free", step)
                            nc.vector.tensor_tensor((LO if kind == "q" else KLO)[s][:, :], dst,
                                                    (HI if kind == "q" else KHI)[s][:, :].bitcast(F32), ALU.subtract)\
                              .then_inc(sems["lo"], 1)
                    elif kind in ("q", "k", "kx"):
                        n = S if kind == "kx" else T
                        hi, lo = (HI[s], LO[s]) if kind == "q" else (KHI[s], KLO[s])
                        done(dve, it, "hi", step)
                        nc.vector.scalar_tensor_tensor(lo[:, 0:n], MISCP[:, 0:n],
                                                       qk_bias(step[2], 0 if kind == "q" else 1),
                                                       hi[:, 0:n].bitcast(F32), ALU.add, ALU.subtract)\
                          .then_inc(sems["misc_free"], 1)
                    if kind == "v":
                        done(dve, it, "misc_full", step)
                        dst = VA[s][:, :, :].rearrange("p t (h c) -> p (t h) c", c=VW)[:, :, 0:DH]
                        src = MISCP[:, :].rearrange("p (t h c) -> p (t h) c", t=TT, c=DH)
                        if step[2] == LIN:
                            nc.vector.tensor_copy(dst, src).then_inc(sems["misc_free"], 1)
                        else:
                            vb = v_bias(step[2])
                            for tt in range(TT):
                                ins = nc.vector.tensor_tensor(
                                    dst[:, tt * H:tt * H + H, :], src[:, tt * H:tt * H + H, :],
                                    vb.rearrange("p (h c) -> p h c", c=DH), ALU.add)
                            ins.then_inc(sems["misc_free"], 1)
                    if kind == "vx":
                        i = 0 if step[2] == X0 else 1
                        done(dve, it, "misc_full", step)
                        vb = v_bias(step[2]).rearrange("p (h c) -> p h c", c=DH)
                        nc.vector.tensor_tensor(VA[s][:, 0, :].rearrange("p (h c) -> p h c", c=VW)[:, :, 0:DH],
                                                MISCP[:, 0:D].rearrange("p (h c) -> p h c", c=DH), vb, ALU.add)
                        tail = MISCP[:, D:2 * D].rearrange("p (g j c) -> p g j c", g=G, j=J)
                        vb = BVM[:, i, :].rearrange("p (g j c) -> p g j c", g=G, j=J)
                        for j in range(J):
                            r = slice(VW * j, VW * j + VW)
                            ins = nc.vector.scalar_tensor_tensor(VT[s][r, :, VW * j:VW * j + DH], tail[r, :, j, :],
                                                                 table["tailmask"][r, :], vb[r, :, j, :],
                                                                 ALU.mult, ALU.add)
                        ins.then_inc(sems["misc_free"], 1)
                    if kind == "state":
                        done(dve, it, "misc_full", step)
                        if step[3] == 0:
                            landed(dve, it, ("q", s, LIN))
                        nc.vector.tensor_tensor(SM[s][:, step[3], :], MISCP[:, :], table["blockdiag"], ALU.mult)\
                          .then_inc(sems["misc_free"], 1)
                    if kind == "lin_scores":
                        _, _, layer, g, p = step
                        place = SCORE_PLACE[step]
                        unit = UNIT_AT[("lin_values", s, layer, g, p)]
                        done(dve, it, "scores_full", step)
                        if unit >= 2:
                            done(dve, it, "values_done", UNITS[unit - 2])
                        for c in range(2):
                            ins = nc.vector.tensor_tensor(
                                PR[:, unit % 2, c, :].rearrange("p (j t) -> p j t", j=J),
                                SC[place][:, c, :].rearrange("p (j t) -> p j t", j=J),
                                spread(table["causal"], J), ALU.mult)
                        ins.then_inc(sems["masked"], 1)
                    if kind == "max":
                        _, _, layer, g, qt, j = step
                        done(dve, it, "max_full", step)
                        place = MAX_PLACE[step]
                        if layer == SELF:
                            src, dst = MX[place][:, :], NEG[s][:, qt, j:j + 1]
                        else:
                            src = MX[place][:, 0:2 * S].rearrange("p (a n) -> p a n", a=2)
                            dst = NEG[s][:, qt, 2 * j:2 * j + 2]
                        nc.vector.tensor_reduce(dst, src, AX.X, ALU.max, negate=True).then_inc(sems["max_free"], 1)
                    if kind == "shift":
                        _, _, layer, g = step
                        last = ("max", s, layer, g, TT - 1, J - 1 if layer == SELF else 1)
                        done(dve, it, "max_free", last)
                        if g:
                            done(dve, it, "misc_free", ("shift", s, layer, g - 1))
                        hi = NMP[s][:, :, ROWS:ROWS + J]
                        link(nc.vector.tensor_copy(hi.bitcast(F32R), NEG[s][:, :, :]))
                        nc.vector.tensor_tensor(NMP[s][:, :, ROWS + J:ROWS + 2 * J].bitcast(F32R), NEG[s][:, :, :], hi,
                                                ALU.subtract).then_inc(sems["shift_split"], 1)
                    if kind == "norm":
                        _, _, layer, tt = step
                        done(dve, it, "misc_full", step)
                        m = MISCP[:, :].rearrange("p (h c) -> p h c", c=VW)
                        den = m[:, :, DH]
                        if layer == LIN:
                            link(nc.vector.tensor_scalar(REC[s][:, :], den, EPS_DEN, None, ALU.add))
                            den = REC[s][:, :]
                        link(nc.vector.reciprocal(REC[s][:, :], den))
                        r = REC[s][:, :]
                        rb = bass.AP(tensor=r.tensor, offset=r.offset, ap=[list(r.ap[0]), [1, H], [0, DH]])
                        nc.vector.tensor_tensor(O[s][:, tt, :].rearrange("p (h c) -> p h c", c=DH), m[:, :, 0:DH], rb,
                                                ALU.mult).then_inc(sems["misc_free"], 1)
                    if kind == "y":
                        layer = step[2]
                        z = Z[s][:, :, :]
                        y = MISCP[:, :].rearrange("p (t d) -> p t d", t=TT)
                        done(dve, it, "misc_full", step)
                        if layer == FFN0:
                            for tt in range(TT):
                                ins = nc.vector.tensor_tensor(Z[s][:, tt, :], y[:, tt, :], F0R[:, 1, :], ALU.add)
                            ins.then_inc(sems["misc_free"], 1)
                            done(dve, it, "misc_free", step)
                            link(nc.vector.tensor_scalar(z, z, MAX_VAL, -MAX_VAL, ALU.min, ALU.max))
                            link(nc.vector.tensor_tensor(z, z, X[s][:, :, :], ALU.add))
                        else:
                            res = X[s] if layer == LIN else XB[s]
                            if layer != LIN:
                                done(dve, it, f"xb{s}", ("y", s, layer - 1))
                            nc.vector.tensor_tensor(z, y, res[:, :, :], ALU.add).then_inc(sems["misc_free"], 1)
                            done(dve, it, "misc_free", step)
                        for tt in range(TT):
                            ins = nc.vector.bn_stats(ST6[s][:, tt, :], Z[s][:, tt, :])
                        link(ins)
                        nc.vector.memset(MARK[:, :], 0.0)
                        for tt in range(TT):
                            ins = nc.vector.bn_aggr(MV[s][:, tt, :], ST6[s][:, tt, :])
                        link(ins)
                        nc.vector.tensor_scalar(VE[s][:, :], MV[s][:, :, 1], EPS_LN, None, ALU.add)\
                          .then_inc(sems[f"var{s}"], 1)
                        done(dve, it, f"rstd{s}", step)
                        for tt in range(TT):
                            ins = nc.vector.tensor_scalar(X[s][:, tt, :], Z[s][:, tt, :], MV[s][:, tt, 0:1],
                                                          RST[s][:, tt:tt + 1], ALU.subtract, ALU.mult)
                        ins.then_inc(sems[f"x{s}"], 1)
                assert chain[0] == CH, chain[0]

        @block.tensor
        def _(pe):
            mm = nc.tensor.matmul
            pe.wait_ge(weights_in, 16 * NW)
            mm(MISCP[:, 0:D], WFR[:, 0, :], table["cos"], start=True, stop=False)
            mm(MISCP[:, 0:D], WFR[:, 1, :], table["sin"], start=False, stop=True)
            mm(MISCP[:, D:2 * D], WFR[:, 1, :], table["cos"], start=True, stop=False)
            mm(MISCP[:, D:2 * D], WFR[:, 0, :], table["nsin"], start=False, stop=True).then_inc(prep_tensor, 1)
            pe.wait_ge(prep_vector, 3)
            mm(MISCP[:, 0:D], GT[:, 0, :], table["cos"], start=True, stop=False)
            mm(MISCP[:, 0:D], GT[:, 1, :], table["nsin"], start=False, stop=True).then_inc(prep_tensor, 1)
            pe.wait_ge(prep_vector, 4)
            pe.wait_ge(prep_gpsimd, N_GPREP)
            pe.wait_ge(prep_vector, N_VPREP)
            pe.wait_ge(aug_in, 16 * NS * G)
            with pe.Fori(0, PAIRS) as it:
                for step in STEPS:
                    kind, s = step[0], step[1]
                    if kind == "xt":
                        if step[2] == LIN:
                            pe.wait_ge(x_in[s], it * 32 + 32)
                        else:
                            done(pe, it, f"x{s}", x_key(s, step[2]))
                        misc_empty(pe, it, step)
                        for tt in range(TT):
                            ins = nc.tensor.transpose(MISCP[:, tt * P:tt * P + P], X[s][:, tt, :], ident)
                        ins.then_inc(sems["misc_full"], 1)
                    if kind in ("q", "k"):
                        misc_empty(pe, it, step)
                        mm(MISCP[:, :], (w_q if kind == "q" else w_k)(step[2]), XT[s][:, :], start=True, stop=True)\
                            .then_inc(sems["misc_full"], 1)
                    if kind == "kx":
                        misc_empty(pe, it, step)
                        pe.wait_ge(x_in[s], it * 32 + 32)
                        mm(MISCP[:, 0:S], w_k(step[2]), CT[s][:, :], start=True, stop=True)\
                            .then_inc(sems["misc_full"], 1)
                    if kind == "vx":
                        misc_empty(pe, it, step)
                        mm(MISCP[:, 0:D], CT[s][:, 0:P], w_v(step[2]), start=True, stop=True)
                        for j in range(J):
                            ins = mm(MISCP[VW * j:VW * j + VW, D:2 * D], CT[s][:, TAIL_AT:S], w_v(step[2]),
                                     start=True, stop=True)
                        ins.then_inc(sems["misc_full"], 1)
                    if kind in ("v", "ktok"):
                        misc_empty(pe, it, step)
                        w = w_v(step[2]) if kind == "v" else w_k(step[2])
                        for tt in range(TT):
                            ins = mm(MISCP[:, tt * D:tt * D + D], XT[s][:, tt * P:tt * P + P], w, start=True, stop=True)
                        ins.then_inc(sems["misc_full"], 1)
                    if kind == "state":
                        c = step[3]
                        misc_empty(pe, it, step)
                        mm(MISCP[:, :], KTOK[s][:, c, :], VA[s][:, c, :], start=(c == 0), stop=True,
                           skip_group_check=True).then_inc(sems["misc_full"], 1)
                    if kind == "lin_scores":
                        _, _, layer, g, p = step
                        if p == 0:
                            if g == 0:
                                landed(pe, it, ("q", s, layer))
                                landed(pe, it, ("k", s, layer))
                        score_empty(pe, it, step)
                        place = SCORE_PLACE[step]
                        for c in range(2):
                            t = slice((2 * p + c) * P, (2 * p + c + 1) * P)
                            for j in range(J):
                                ins = mm(SC[place][:, c, j * P:j * P + P], KM[s][0:ROWS, g, j, t], QS[s][0:ROWS, g, t],
                                         start=True, stop=True)
                        ins.then_inc(sems["scores_full"], 1)
                    if kind == "lin_values":
                        _, _, layer, g, p = step
                        unit = UNIT_AT[step]
                        done(pe, it, "masked", ("lin_scores", s, layer, g, p))
                        if p == 0:
                            heads_out_free(pe, it, step)
                            if g == 0:
                                done(pe, it, "misc_free", ("state", s, layer, TT - 2))
                        for c in range(2):
                            n = 2 * p + c
                            t = slice(n * P, n * P + P)
                            if n:
                                mm(OTP[:, t], SM[s][:, n - 1, g * P:g * P + P], QF[s][:, t], start=True, stop=False,
                                   skip_group_check=True)
                            for j in range(J):
                                h = g * J + j
                                ins = mm(OTP[VW * j:VW * j + VW, t], VA[s][:, n, h * VW:h * VW + VW],
                                         PR[:, unit % 2, c, j * P:j * P + P], start=(n == 0), stop=True,
                                         skip_group_check=True)
                        ins.then_inc(sems["values_done"], 1)
                    if kind == "max":
                        _, _, layer, g, qt, j = step
                        if qt == 0 and j == 0:
                            if g == 0:
                                landed(pe, it, ("q", s, layer))
                                landed(pe, it, ("k" if layer == SELF else "kx", s, layer))
                        if MAX_LAST[step] is not None:
                            done(pe, it, "max_free", MAX_LAST[step])
                        else:
                            earlier(pe, it, "max_free")
                        place = MAX_PLACE[step]
                        q = QS[s][0:ROWS, g, qt * P:qt * P + P]
                        if layer == SELF:
                            ins = mm(MX[place][:, :], q, KM[s][0:ROWS, g, j, :], start=True, stop=True)
                        else:
                            ins = mm(MX[place][:, 0:2 * S].rearrange("p (a n) -> p a n", a=2), q,
                                     KM[s][0:ROWS, g, 2 * j:2 * j + 2, 0:S], start=True, stop=True)
                        ins.then_inc(sems["max_full"], 1)
                    if kind == "shift":
                        done(pe, it, "shift_split", step)
                        misc_empty(pe, it, step)
                        for qt in range(TT):
                            ins = nc.tensor.transpose(MISCP[:, qt * P:qt * P + P], NMP[s][:, qt, :], ident)
                        ins.then_inc(sems["misc_full"], 1)
                    if kind == "scores":
                        _, _, layer, g, kt, half = step
                        if kt == 0 and half == 0:
                            done(pe, it, "misc_free", ("shift", s, layer, g))
                        score_empty(pe, it, step)
                        place = SCORE_PLACE[step]
                        for a in range(2):
                            ins = mm(SC[place][:, a, :], KM[s][:, g, 2 * half + a, kt * P:kt * P + P], QS[s][:, g, :],
                                     start=True, stop=True)
                        ins.then_inc(sems["scores_full"], 1)
                    if kind == "values":
                        _, _, layer, g, kt = step
                        unit = UNIT_AT[step]
                        done(pe, it, "probs", ("scores", s, layer, g, kt, 1))
                        if kt == 0:
                            heads_out_free(pe, it, step)
                            if g == 0:
                                done(pe, it, "misc_free", ("v", s, layer))
                        for j in range(J):
                            h = g * J + j
                            ins = mm(OTP[VW * j:VW * j + VW, :], VA[s][:, kt, h * VW:h * VW + VW],
                                     PR[:, unit % 2, j, :], start=(kt == 0), stop=(kt == TT - 1))
                        ins.then_inc(sems["values_done"], 1)
                    if kind == "xscores":
                        _, _, layer, g, part = step
                        if part == 0:
                            done(pe, it, "misc_free", ("shift", s, layer, g))
                            if g == 0:
                                done(pe, it, "tail", ("kx", s, layer))
                        score_empty(pe, it, step)
                        place = SCORE_PLACE[step]
                        if part < 2:
                            for a in range(2):
                                ins = mm(SC[place][:, a, :], KM[s][:, g, 2 * part + a, 0:P], QS[s][:, g, :],
                                         start=True, stop=True)
                        else:
                            ins = mm(SC[place][:, 0, :], KT[s][:, g, :], QS[s][:, g, :], start=True, stop=True)
                        ins.then_inc(sems["scores_full"], 1)
                    if kind == "xvalues":
                        _, _, layer, g = step
                        unit = UNIT_AT[step]
                        done(pe, it, "probs", ("xscores", s, layer, g, 2))
                        heads_out_free(pe, it, step)
                        if g == 0:
                            done(pe, it, "misc_free", ("vx", s, layer))
                        mm(OTP[:, :], VT[s][:, g, :], PT[:, unit % 2, :], start=True, stop=False,
                           skip_group_check=True)
                        for j in range(J):
                            h = g * J + j
                            ins = mm(OTP[VW * j:VW * j + VW, :], VA[s][:, 0, h * VW:h * VW + VW], PR[:, unit % 2, j, :],
                                     start=False, stop=True, skip_group_check=True)
                        ins.then_inc(sems["values_done"], 1)
                    if kind == "norm":
                        _, _, layer, tt = step
                        misc_empty(pe, it, step)
                        done(pe, it, "heads_out", next(x for x in HEADS_OUT if x[1:4] == (s, layer, G - 1)))
                        for g in range(G):
                            ins = nc.tensor.transpose(MISCP[:, g * P:g * P + P], OT[s][:, g, tt * P:tt * P + P], ident)
                        ins.then_inc(sems["misc_full"], 1)
                    if kind == "turn":
                        misc_empty(pe, it, step)
                        for tt in range(TT):
                            ins = nc.tensor.transpose(MISCP[:, tt * P:tt * P + P], O[s][:, tt, :], ident)
                        ins.then_inc(sems["misc_full"], 1)
                    if kind == "y":
                        layer = step[2]
                        misc_empty(pe, it, step)
                        src = XT[s] if layer in (FFN0, FFN1) else OC[s]
                        for tt in range(TT):
                            ins = mm(MISCP[:, tt * D:tt * D + D], src[:, tt * P:tt * P + P], w_out(layer),
                                     start=True, stop=True)
                        ins.then_inc(sems["misc_full"], 1)


def kernel(**inputs):
    import numpy as _np
    import concourse.bacc as _bacc
    from concourse import mybir as _mybir
    from concourse.bass_utils import run_bass_kernel_spmd as _run

    a = {k: _np.asarray(v) for k, v in inputs.items()}
    cross = lambda pre, q, k, v, o: _np.stack([a[pre + n].T for n in (q, k, v, o)], axis=1)
    arrays = {
        "x": a["x"],
        "ctxT": a["ctx_1024"].transpose(0, 2, 1),
        "w_lin": a["L0_attn_w_attn"],
        "w_lin_proj": a["L0_attn_w_proj"],
        "wx0": cross("L0_xattn_W", "q", "k", "v", "o"),
        "bx0": _np.stack([a["L0_xattn_bq"], a["L0_xattn_bk"]], axis=1),
        "bx0_row": _np.stack([a["L0_xattn_bv"], a["L0_xattn_bo"]]),
        "w_ffn0": a["L0_ffn_weights"].T,
        "ffn0_row": _np.stack([a["L0_ffn_scale"], a["L0_ffn_bias"]]),
        "w_self": a["L1_attn_w_qkv"],
        "b_self": a["L1_attn_b_qkv"].reshape(3, D)[0:2].T,
        "b_self_row": _np.stack([a["L1_attn_b_qkv"][2 * D:], a["L1_attn_b_out"]]),
        "w_self_out": a["L1_attn_w_out"],
        "wx1": cross("L1_xattn_w_", "q", "k", "v", "o"),
        "bx1": _np.stack([a["L1_xattn_b_q"], a["L1_xattn_b_k"]], axis=1),
        "bx1_row": _np.stack([a["L1_xattn_b_v"], a["L1_xattn_b_o"]]),
        "w_freq": _np.stack([a["L1_ffn_w_freq_real"], a["L1_ffn_w_freq_imag"]], axis=1),
        "ffn1_row": a["L1_ffn_bias"],
        "const": CONST,
    }
    arrays = {f"in_{k}_dram": _np.ascontiguousarray(v) for k, v in arrays.items()}
    nc = _bacc.Bacc("TRN2", target_bir_lowering=False, num_devices=1)
    args = [nc.dram_tensor(k, v.shape, _mybir.dt.from_np(v.dtype), kind="ExternalInput").ap()
            for k, v in arrays.items()]
    args.append(nc.dram_tensor("out_0_dram", (B, T, D), _mybir.dt.from_np(_np.dtype("float32")),
                               kind="ExternalOutput").ap())
    build(nc, *args)
    r = _run(nc, [arrays], core_ids=[0])
    return r.results[0]["out_0_dram"]
```

```python
from contextlib import ExitStack

import numpy as np

import concourse.bass as bass
from concourse import mybir

F32 = mybir.dt.float32
F32R = mybir.dt.float32r
ACT = mybir.ActivationFunctionType
ALU = mybir.AluOpType
AX = mybir.AxisListType

P = 128
B, T, D = 4, 512, 128
S = 154
H, DH = 16, 8
G, J = 4, 4
TT = T // P
SPLIT = 32
ROWS = 3 * SPLIT
VW = 32
HALF = VW // 2
GROUPS = (0, 2, 1, 3)
TAIL = 32
TAIL_AT = S - TAIL
NS = 2
PAIRS = B // NS
SCALE = float(DH) ** -0.5
EPS_LN = 1e-5
EPS_DEN = 1e-6
MAX_VAL = 100.0

LIN, X0, FFN0, SELF, X1, FFN1 = range(6)
ATTN = (LIN, X0, SELF, X1)


def constants():
    r = np.arange(P)
    k = 2 * np.pi * ((r[:, None] * r[None, :]) % D) / D
    parts = {
        "ident": np.eye(P),
        "cos": np.cos(k),
        "sin": np.sin(k),
        "nsin": -np.sin(k),
        "causal": (r[:, None] <= r[None, :]),
        "headmask": (r[:, None] % SPLIT // DH == np.arange(J)[None, :]),
        "augmask": (r[:, None] >= ROWS) & (r[:, None] < ROWS + 2 * J) & (r[:, None] % J == np.arange(J)[None, :]),
        "tailmask": (r[:, None] % TAIL >= P - TAIL_AT),
        "eps": EPS_DEN * (r[:, None] % HALF == DH),
        "blockdiag": (r[:, None] // DH == np.arange(H * VW)[None, :] // VW),
    }
    at, out = {}, []
    n = 0
    for name, a in parts.items():
        at[name] = (n, n + a.shape[1])
        n += a.shape[1]
        out.append(a.astype(np.float32))
    return at, np.ascontiguousarray(np.concatenate(out, axis=1))


CONST_AT, CONST = constants()


def attention_steps(s, layer):
    shifts, scores, values = [], [], []
    for place, g in enumerate(GROUPS):
        if layer == LIN:
            scores += [("lin_scores", s, layer, g, p) for p in range(2)]
            values += [("lin_values", s, layer, g, p) for p in range(2)]
            continue
        shifts += [("max", s, layer, g, qt, j) for qt in range(TT) for j in range(J if layer == SELF else 2)]
        shifts += [("split", s, layer, g), ("shift", s, layer, g)]
        if layer == SELF:
            scores += [("scores", s, layer, g, kt, half) for kt in range(TT) for half in range(2)]
            values += [("values", s, layer, g, kt) for kt in range(TT)]
        else:
            scores += [("xscores", s, layer, g, part) for part in range(3)]
            values += [("xvalues", s, layer, g)]
    return shifts, scores, values


def unit_of(step):
    kind, s, layer, g = step[:4]
    return {"scores": ("values", s, layer, g, step[4]), "xscores": ("xvalues", s, layer, g),
            "lin_scores": ("lin_values", s, layer, g, step[4])}[kind]


def needs(step):
    kind, s = step[:2]
    if kind == "load":
        return []
    layer = step[2] if kind != "store" else FFN1
    q, k, v = [(n, s, layer) for n in (("q", "kx", "vx") if layer in (X0, X1) else ("q", "k", "v"))]
    if kind == "xt":
        return [("load", s) if layer == LIN else ("ln", s, layer - 1)]
    if kind == "kx":
        return [attention_steps(s, layer - 1)[1][-1]]
    if kind == "vx":
        return [attention_steps(s, layer - 1)[2][-1]]
    if kind in ("q", "k", "v", "ktok"):
        return [("xt", s, layer)]
    if kind == "state":
        return [v, q, ("ktok", s, layer)] + ([("state", s, layer, step[3] - 1)] if step[3] else [])
    if kind in ("max", "lin_scores"):
        return [q, k]
    if kind == "split":
        g = step[3]
        place = GROUPS.index(g)
        return [("max", s, layer, g, TT - 1, J - 1 if layer == SELF else 1)] + \
               ([("shift", s, layer, GROUPS[place - 2])] if place >= 2 else [])
    if kind == "shift":
        return [("split", s, layer, step[3])]
    if kind in ("scores", "xscores"):
        return [("shift", s, layer, step[3]), k]
    if kind == "values":
        return [("scores", *step[1:], 1), v]
    if kind == "xvalues":
        return [("xscores", *step[1:], 2), v]
    if kind == "lin_values":
        return [("lin_scores", *step[1:]), ("state", s, layer, TT - 2)]
    if kind == "norm":
        last = G // 2 + step[3]
        return [("xvalues", s, layer, last) if layer in (X0, X1) else
                ("values", s, layer, last, TT - 1) if layer == SELF else ("lin_values", s, layer, last, 1)]
    if kind == "y":
        return [("xt" if layer in (FFN0, FFN1) else "turn", s, layer)]
    if kind == "turn":
        return [("norm", s, layer, b) for b in range(G // 2)]
    if kind in ("ln", "store"):
        return [("y" if kind == "ln" else "ln", s, layer)]
    raise ValueError(kind)


def stages(step):
    kind = step[0]
    lin = len(step) > 2 and step[2] == LIN
    if kind == "load":
        return [("queue", 2.5)], 0
    if kind == "store":
        return [("queue", 2.0)], 0
    if kind in ("xt", "turn"):
        return [("pe", .9), ("act", .5)], 1
    if kind == "q":
        return ([("pe", .9), ("dve", .6), ("act", .5), ("dve", .6), ("act", .5), ("dve", .4), ("dma", 5.)], 3) if lin \
            else ([("pe", .9), ("act", .5), ("dve", .6), ("dma", 5.)], 2)
    if kind == "k":
        return ([("pe", .9), ("dve", .6), ("act", .5), ("dve", .6), ("act", .5), ("dve", .4), ("dma", 9.)], 3) if lin \
            else ([("pe", .9), ("act", .5), ("dve", .6), ("dma", 9.)], 2)
    if kind == "kx":
        return [("pe", .3), ("act", .3), ("dve", .3), ("dma", 8.), ("pool", 1.)], 2
    if kind == "ktok":
        return [("pe", .9), ("dve", .6), ("act", .5), ("dve", .6)], 3
    if kind == "v":
        return [("pe", .9), ("dve", .9)], 1
    if kind == "vx":
        return [("pe", .7), ("dve", 1.5)], 1
    if kind == "state":
        return [("pe", .9), ("dve", .65)], 1
    if kind == "max":
        return [("pe", .22 if step[2] == SELF else .14), ("dve", .58 if step[2] == SELF else .4)], 1
    if kind == "split":
        return [("dve", .5)], 0
    if kind == "shift":
        return [("pe", .28), ("act", .4)], 1
    if kind in ("scores", "xscores"):
        return ([("pe", .22), ("act", .5)], 1) if kind == "xscores" and step[4] == 2 else \
               ([("pe", .44), ("act", .93)], 1)
    if kind == "lin_scores":
        return [("pe", .6), ("dve", 1.2)], 1
    if kind in ("values", "xvalues", "lin_values"):
        return ([("pe", .9), ("act", .5)] if ("heads_out", step) in signals(step) else [("pe", .9)]), 0
    if kind == "norm":
        return [("pe", .9), ("dve", .75)], 1
    if kind == "y":
        return [("pe", .9), ("dve", 2.), ("pool", .4)], 1
    if kind == "ln":
        return [("dve", .6)], 0
    raise ValueError(kind)


def plan():
    sequences = []
    for s in range(NS):
        chain = [("load", s)]
        for layer in ATTN:
            names = {LIN: ("xt", "k", "q", "v", "ktok"), SELF: ("xt", "k", "q", "v")}.get(layer, ("xt", "q"))
            chain += [(n, s, layer) for n in names]
            if layer == LIN:
                chain += [("state", s, layer, c) for c in range(TT - 1)]
            chain += [("norm", s, layer, b) for b in range(G // 2)] + \
                     [("turn", s, layer), ("y", s, layer), ("ln", s, layer)]
            if layer in (X0, X1):
                chain += [("xt", s, layer + 1), ("y", s, layer + 1), ("ln", s, layer + 1)]
        chain.append(("store", s))
        sequences += [chain, [(n, s, layer) for layer in (X0, X1) for n in ("kx", "vx")]]
        parts = [attention_steps(s, layer) for layer in ATTN]
        sequences += [[x for part in parts for x in part[n]] for n in range(3)]
    every = [x for seq in sequences for x in seq]
    users = {x: [] for x in every}
    for x in every:
        for y in needs(x):
            users[y].append(x)
    for seq in sequences:
        if seq[0][0] not in ("load", "kx"):
            for a, b in zip(seq, seq[1:]):
                users[a].append(b)
    way = {}

    def length(x):
        if x not in way:
            way[x] = sum(t for _, t in stages(x)[0]) + max((length(u) for u in users[x]), default=0.0)
        return way[x]

    free = dict.fromkeys(("pe", "act", "dve", "pool", "dma", "queue"), 0.0)
    score_free, heads_free = [0.0, 0.0], 0.0
    bank_free, bank_of = [0.0] * BANKS, {}
    summing = None
    end, opened, units_done = {}, [], 0
    scores_left = {}
    for x in every:
        if x[0] in SCORES_KINDS:
            scores_left[bank_id(x)] = scores_left.get(bank_id(x), 0) + 1
    out = []

    def times(step):
        parts, frees = stages(step)
        t = max((end[x] for x in needs(step)), default=0.0) + LAG
        bank = None
        if step[0] in SCORES_KINDS:
            t = max(t, score_free[0] + LAG)
        if step[0] in BANK_KINDS:
            if step[0] == "state" and step[3]:
                bank = bank_of["state", step[1], LIN, step[3] - 1]
            else:
                bank = min((b for b in range(BANKS) if b != summing), key=lambda b: bank_free[b])
            t = max(t, bank_free[bank] + LAG)
        if step in HEADS_START:
            t = max(t, heads_free + LAG)
        begun, begin = [], None
        now = dict(free)
        for n, (eng, dur) in enumerate(parts):
            start = max(t, now[eng])
            if n == 0:
                begin = start
            t = start + dur
            now[eng] = t
            begun.append(t)
            t += LAG
        return begin, bank, begun, now, frees

    heads = [list(seq) for seq in sequences]
    while any(heads):
        best = None
        for n, seq in enumerate(heads):
            if not seq:
                continue
            x = seq[0]
            if any(y not in end for y in needs(x)):
                continue
            if x[0] in SCORES_KINDS:
                u = unit_of(x)
                if u not in opened and (len(opened) >= units_done + 2 or (
                        opened and bank_id(opened[-1]) != bank_id(x) and scores_left[bank_id(opened[-1])])):
                    continue
            if x[0] in VALUES_KINDS and opened[units_done] != x:
                continue
            if x[0] == "state" and x[3] == 0 and summing is not None:
                continue
            begin, bank, begun, now, frees = times(x)
            key = begin - LEAD.get(x[0], LEAD["chain"]) - WAY * length(x) - (x[1] == 0) * LEAD["first"]
            if best is None or key < best[0]:
                best = (key, n, x, bank, begun, now, frees)
        assert best, [h[0] for h in heads if h]
        _, n, x, bank, begun, now, frees = best
        heads[n].pop(0)
        free.update(now)
        end[x] = begun[-1]
        if bank is not None:
            bank_free[bank], bank_of[x] = begun[frees], bank
            if x[0] == "state":
                summing = bank if x[3] < TT - 2 else None
        if x[0] in SCORES_KINDS:
            if unit_of(x) not in opened:
                opened.append(unit_of(x))
            scores_left[bank_id(x)] -= 1
            score_free = score_free[1:] + [begun[frees]]
        if x[0] in VALUES_KINDS:
            units_done += 1
            if ("heads_out", x) in signals(x):
                heads_free = begun[-1]
        out.append(x)
    return out, bank_of, max(end.values())


BANKS = 3
BANK_KINDS = ("max", "xt", "q", "k", "kx", "v", "vx", "ktok", "state", "shift", "norm", "turn", "y")
VALUES_KINDS = ("values", "lin_values", "xvalues")
SCORES_KINDS = ("scores", "xscores", "lin_scores")
HEADS_START = {x for s in range(NS) for layer in ATTN for x in attention_steps(s, layer)[2]
               if x[3] < G // 2 and (len(x) == 4 or x[4] == 0)}


def bank_id(step):
    return step[1], step[2], step[3] % 2


LAG = .2
WAY = 0
LEAD = {"chain": 0, "first": 0, "max": 0.05, "split": 2.9, "shift": 0.42, "scores": 0,
        "xscores": 0, "lin_scores": 0, "values": 0, "xvalues": 0.11, "lin_values": 0.31}


BIAS_AFTER = {LIN: X0, FFN0: SELF, SELF: X1, X1: FFN1}


def freed(step):
    return "act_freed" if step[0] in ("xt", "turn", "shift") else "dve_freed"


def signals(step):
    kind, rest = step[0], step[1:]
    s = rest[0]
    if kind in BANK_KINDS:
        out = [("bank_full", step), (freed(step), step)]
        if kind in ("q", "k", "ktok") and rest[1] == LIN:
            out += [("clipped", step), ("exped", step)]
        if kind in ("q", "k", "kx"):
            out.append(("hi", step))
        if kind in ("q", "k") and rest[1] == LIN:
            out.append(("lo", step))
        if kind == "kx":
            out.append(("tail", step))
        if kind == "y":
            out += [(f"var{s}", step), (f"rstd{s}", step)]
        return out
    if kind == "split":
        return [("shift_split", step)]
    if kind in ("scores", "xscores"):
        return [("scores_full", step), ("probs", step)]
    if kind == "lin_scores":
        return [("scores_full", step), ("masked", step)]
    if kind in ("values", "lin_values", "xvalues"):
        out = [("values_done", step)]
        if rest[2] >= G // 2 and (kind == "xvalues" or rest[3] == (TT if kind == "values" else 2) - 1):
            out.append(("heads_out", step))
        return out
    if kind == "ln":
        out = [(f"x{s}", step)]
        if rest[1] in BIAS_AFTER:
            out.append((f"xb{s}", step))
        return out
    return []


STEPS, BANK_OF, _ = plan()


def count():
    value, total = {}, {}
    for step in STEPS:
        for name, key in signals(step):
            total[name] = total.get(name, 0) + 1
            value[name, key] = total[name]
    return value, total


VALUE, TOTAL = count()


def ring(kinds, size):
    place, last, n, held = {}, {}, 0, [None] * size
    for step in STEPS:
        if step[0] in kinds:
            place[step] = n % size
            last[step] = held[n % size]
            held[n % size] = step
            n += 1
    return place, last, held


SCORE_PLACE, SCORE_LAST, SCORE_HELD = ring(("scores", "xscores", "lin_scores"), 2)
BANK_LAST, BANK_HELD = {}, [None] * BANKS
for step in STEPS:
    if step in BANK_OF:
        BANK_LAST[step] = BANK_HELD[BANK_OF[step]]
        BANK_HELD[BANK_OF[step]] = step
UNITS = [x for x in STEPS if x[0] in VALUES_KINDS]
UNIT_AT = {x: n for n, x in enumerate(UNITS)}
HEADS_OUT = [x for x in UNITS if ("heads_out", x) in signals(x)]
HEADS_LAST = {b: a for a, b in zip(HEADS_OUT, HEADS_OUT[1:])}
PRIMED = ("act_freed", "dve_freed", "probs", "masked", "heads_out", "x0", "x1")
K_STEPS = [[x for x in STEPS if x[0] in ("k", "kx") and x[1] == s] for s in range(NS)]
K_LAST = {b: a for steps in K_STEPS for a, b in zip(steps, steps[1:])}


def bank_end(s, layer, b):
    return next(x for x in HEADS_OUT if bank_id(x) == (s, layer, b))


def chain_length():
    n = 0
    for step in STEPS:
        if step[0] == "split":
            n += 1
        if step[0] == "norm":
            n += 1
        if step[0] == "y":
            n += 4 if step[2] == FFN0 else 2
    return n


DVE_CHAIN = chain_length()


def build(nc, x, ctxT, w_lin, w_lin_proj, wx0, bx0, bx0_row, w_ffn0, ffn0_row, w_self, b_self, b_self_row, w_self_out,
          wx1, bx1, bx1_row, w_freq, ffn1_row, const, out):
    with ExitStack() as ctx:
        def sb(name, shape, dt=F32):
            return ctx.enter_context(nc.sbuf_tensor(name, shape, dt))

        def sem(name):
            return ctx.enter_context(nc.semaphore(name))

        C = sb("C", [P, CONST.shape[1]])
        table = {name: C[:, a:b] for name, (a, b) in CONST_AT.items()}
        ident = table["ident"]
        WL = sb("WL", [P, 3 * D])
        WLP = sb("WLP", [P, D])
        WX = [sb(f"WX{i}", [P, 4, D]) for i in range(2)]
        BX = [sb(f"BX{i}", [P, 2]) for i in range(2)]
        BXR = [sb(f"BXR{i}", [P, 2, D]) for i in range(2)]
        WS = sb("WS", [P, 3 * D])
        BS = sb("BS", [P, 2])
        BSR = sb("BSR", [P, 2, D])
        WSO = sb("WSO", [P, D])
        WF0 = sb("WF0", [P, D])
        F0R = sb("F0R", [P, 2, D])
        WFR = sb("WFR", [P, 2, D])
        F1R = sb("F1R", [P, D])
        WF1 = sb("WF1", [P, D])
        GT = sb("GT", [P, 2, D])
        identr = sb("identr", [P, P], F32R)
        zeros = sb("zeros", [P, T])
        halves = sb("halves", [P, TT])

        def each(name, shape, dt=F32):
            return [sb(f"{name}{s}", shape, dt) for s in range(NS)]

        X = each("X", [P, TT, D])
        XB = each("XB", [P, TT, D])
        XT = each("XT", [P, T])
        CT = each("CT", [P, S])
        SM = each("SM", [P, TT - 1, H * VW])
        QS = each("QS", [P, G, T], F32R)
        KM = each("KM", [P, G, J, T], F32R)
        KT = each("KT", [P, G, J * TAIL], F32R)
        VA = each("VA", [P, TT, H * VW])
        VT = each("VT", [P, G, J * VW])
        OT = each("OT", [P, G // 2, T])
        OC = each("OC", [P, T])
        NEG = each("NEG", [P, G, TT, J])
        NMP = [[sb(f"NMP{s}{i}", [P, TT, P], F32R) for i in range(2)] for s in range(NS)]
        O = each("O", [P, TT, D])
        Z = each("Z", [P, TT, D])
        ST6 = each("ST6", [P, TT, 6])
        MV = each("MV", [P, TT, 2])
        VE = each("VE", [P, TT])
        RST = each("RST", [P, TT])
        REC = each("REC", [P, 2, 2 * H])
        QF = [OC[s][:, :] for s in range(NS)]
        KF = [OT[s][:, 0, :] for s in range(NS)]
        KTOK = [OT[s][:, 1, :].rearrange("p (t d) -> p t d", t=TT) for s in range(NS)]
        T1 = [XB[s][:, :, :].rearrange("p t d -> p (t d)") for s in range(NS)]
        T2 = [SM[s][:, TT - 2, :] for s in range(NS)]
        HI = [SM[s][:, 0, :].bitcast(F32R) for s in range(NS)]
        LO = [SM[s][:, 1, :].bitcast(F32R) for s in range(NS)]
        KHI = [Z[s][:, :, :].rearrange("p t d -> p (t d)").bitcast(F32R) for s in range(NS)]
        KLO = [O[s][:, :, :].rearrange("p t d -> p (t d)").bitcast(F32R) for s in range(NS)]
        KXH = each("KXH", [P, S], F32R)
        KXL = each("KXL", [P, S], F32R)
        SPLITS = {"q": (HI, LO), "k": (KHI, KLO), "kx": (KXH, KXL)}
        MARK = sb("MARK", [P, 1])
        PR = sb("PR", [P, 2, J, T])
        PT = sb("PT", [P, 2, T])
        BVM = sb("BVM", [P, 2, D])

        SC = [ctx.enter_context(nc.psum_tensor(f"SC{i}", [P, 2, T], F32)) for i in range(2)]
        BANK = [ctx.enter_context(nc.psum_tensor(f"BANK{i}", [P, T], F32)) for i in range(BANKS)]
        OTP = ctx.enter_context(nc.psum_tensor("OTP", [P, T], F32))

        QD = [nc.dram_tensor(f"QD{s}", (2, P, T), F32, kind="Internal").ap() for s in range(NS)]
        KD = [nc.dram_tensor(f"KD{s}", (2, P, T), F32, kind="Internal").ap() for s in range(NS)]

        sems = {name: sem(name) for name in TOTAL}
        weights_in = sem("weights_in")
        prep_gpsimd = sem("prep_gpsimd")
        prep_vector = sem("prep_vector")
        prep_tensor = sem("prep_tensor")
        x_in = [sem(f"x_in{s}") for s in range(NS)]
        q_in = [sem(f"q_in{s}") for s in range(NS)]
        q_out = [sem(f"q_out{s}") for s in range(NS)]
        k_out = [sem(f"k_out{s}") for s in range(NS)]
        k_in = [sem(f"k_in{s}") for s in range(NS)]
        stored = [sem(f"stored{s}") for s in range(NS)]
        dve_self = sem("dve_self")
        aug_in = sem("aug_in")

        def done(eng, it, name, key):
            eng.wait_ge(sems[name], it * TOTAL[name] + VALUE[name, key] + (name in PRIMED))

        def earlier(eng, it, name):
            assert name in PRIMED
            eng.wait_ge(sems[name], it * TOTAL[name] + 1)

        def ready(eng, it, step, *inputs):
            level = {}
            for x in inputs:
                level[freed(x)] = max(level.get(freed(x), 0), VALUE[freed(x), x])
            last = BANK_LAST[step]
            if last is not None:
                level[freed(last)] = max(level.get(freed(last), 0), VALUE[freed(last), last])
            else:
                name = freed(BANK_HELD[BANK_OF[step]])
                level[name] = max(level.get(name, 0), 0)
            for name, value in level.items():
                eng.wait_ge(sems[name], it * TOTAL[name] + value + 1)

        def score_empty(eng, it, step):
            last = SCORE_LAST[step]
            if last is None:
                earlier(eng, it, "probs")
                earlier(eng, it, "masked")
            else:
                done(eng, it, "masked" if last[0] == "lin_scores" else "probs", last)

        def heads_out_free(eng, it, unit):
            end = bank_end(*bank_id(unit))
            if end in HEADS_LAST:
                done(eng, it, "heads_out", HEADS_LAST[end])
            else:
                earlier(eng, it, "heads_out")

        def v_columns(tile, at, n):
            first = tile[:, at:at + 1]
            return bass.AP(tensor=tile.tensor, offset=first.offset,
                           ap=[list(tile.ap[0]), [H // 2 * VW + HALF, 2], [VW, H // 2], [1, n]])

        def x_key(s, layer):
            return ("ln", s, layer - 1)

        def w_q(layer):
            return {LIN: WL[:, 0:D], SELF: WS[:, 0:D], X0: WX[0][:, 0, :], X1: WX[1][:, 0, :]}[layer]

        def w_k(layer):
            return {LIN: WL[:, D:2 * D], SELF: WS[:, D:2 * D], X0: WX[0][:, 1, :], X1: WX[1][:, 1, :]}[layer]

        def w_v(layer):
            return {LIN: WL[:, 2 * D:], SELF: WS[:, 2 * D:], X0: WX[0][:, 2, :], X1: WX[1][:, 2, :]}[layer]

        def w_out(layer):
            return {LIN: WLP[:, :], SELF: WSO[:, :], X0: WX[0][:, 3, :], X1: WX[1][:, 3, :],
                    FFN0: WF0[:, :], FFN1: WF1[:, :]}[layer]

        def qk_bias(layer, which):
            return {SELF: BS, X0: BX[0], X1: BX[1]}[layer][:, which:which + 1]

        def v_bias(layer):
            return {SELF: BSR, X0: BXR[0], X1: BXR[1]}[layer][:, 0, :]

        def out_bias(layer):
            return {SELF: BSR[:, 1, :], X0: BXR[0][:, 1, :], X1: BXR[1][:, 1, :], FFN1: F1R[:, :]}[layer]

        def spread(row, n):
            return bass.AP(tensor=row.tensor, offset=row.offset, ap=[list(row.ap[0]), [0, n], list(row.ap[-1])])

        LOADS = {}
        loads_total = {}
        for step in STEPS:
            if step[0] in ("q", "k", "kx"):
                name = ("q" if step[0] == "q" else "k", step[1])
                loads_total[name] = loads_total.get(name, 0) + 1
                LOADS[step] = loads_total[name]

        def landed(eng, it, step):
            name = ("q" if step[0] == "q" else "k", step[1])
            s = step[1]
            eng.wait_ge(q_in[s] if step[0] == "q" else k_in[s],
                        (it * loads_total[name] + LOADS[step]) * 16 * (3 if step[0] == "q" else 3 * J))

        NW = 17
        N_GPREP = 2 + NS * 5 + 1
        N_VPREP = 5 + 2 + J * (1 + 3 * NS)
        block = ctx.enter_context(nc.Block())

        @block.sync
        def _(sp):
            row = lambda r: bass.AP(tensor=r.tensor, offset=r.offset, ap=[[0, P]] + [list(a) for a in r.ap])
            for dst, src in ((C[:, :], const), (WL[:, :], w_lin), (WLP[:, :], w_lin_proj),
                             (WX[0][:, :, :], wx0), (WX[1][:, :, :], wx1), (BX[0][:, :], bx0), (BX[1][:, :], bx1),
                             (BXR[0][:, :, :], row(bx0_row)), (BXR[1][:, :, :], row(bx1_row)),
                             (WS[:, :], w_self), (BS[:, :], b_self), (BSR[:, :, :], row(b_self_row)),
                             (WSO[:, :], w_self_out), (WF0[:, :], w_ffn0), (F0R[:, :, :], row(ffn0_row)),
                             (WFR[:, :, :], w_freq), (F1R[:, :], row(ffn1_row))):
                sp.dma_start(dst, src).then_inc(weights_in, 16)
            sp.wait_ge(prep_vector, N_VPREP)
            for s in range(NS):
                for g in range(G):
                    sp.dma_start(KM[s][ROWS:P, g, :, :].bitcast(F32), PR[ROWS:P, 0, :, :]).then_inc(aug_in, 16)
            sp.wait_ge(prep_gpsimd, N_GPREP)
            with sp.Fori(0, PAIRS) as it:
                for step in STEPS:
                    kind, s = step[0], step[1]
                    if kind in ("q", "k", "kx"):
                        done(sp, it, "lo" if step[2] == LIN else "dve_freed", step)
                        n = S if kind == "kx" else T
                        hi, lo = [part[s] for part in SPLITS[kind]]
                        name, out_sem, in_sem, dram = ("q", q_out[s], q_in[s], QD[s]) if kind == "q" else \
                                                      ("k", k_out[s], k_in[s], KD[s])
                        sp.dma_start(dram[0, :, 0:n], hi[:, 0:n].bitcast(F32)).then_inc(out_sem, 16)
                        sp.dma_start(dram[1, :, 0:n], lo[:, 0:n].bitcast(F32)).then_inc(out_sem, 16)
                        sp.wait_ge(out_sem, (it * loads_total[name, s] + LOADS[step]) * 32)
                        if kind == "q":
                            for blk, part in enumerate((0, 0, 1)):
                                r = slice(SPLIT * blk, SPLIT * blk + SPLIT)
                                sp.dma_start(QS[s][r, :, :].bitcast(F32),
                                             dram[part].rearrange("(g r) t -> r g t", g=G)).then_inc(in_sem, 16)
                            continue
                        for j in range(J):
                            for blk, part in enumerate((0, 1, 0)):
                                r = SPLIT * blk + DH * j
                                src = dram[part].rearrange("(g j d) t -> j d g t", g=G, j=J)[j, :, :, 0:n]
                                sp.dma_start(KM[s][r:r + DH, :, j, 0:n].bitcast(F32), src).then_inc(in_sem, 16)

        @block.gpsimd
        def _(pool):
            n0 = 0
            for ap, v in [(zeros[:, :], 0.0), (halves[:, :], -0.5)]:
                nc.gpsimd.memset(ap, v).then_inc(prep_gpsimd, 1)
                n0 += 1
            for s in range(NS):
                for ap in (KM[s][0:ROWS, :, :, :].bitcast(F32), VA[s][:, :, :], VT[s][:, :, :],
                           NMP[s][0][:, :, :].bitcast(F32), NMP[s][1][:, :, :].bitcast(F32)):
                    nc.gpsimd.memset(ap, 0.0).then_inc(prep_gpsimd, 1)
                    n0 += 1
            pool.wait_ge(prep_gpsimd, n0)
            pool.wait_ge(weights_in, 16 * NW)
            last = None
            for s in range(NS):
                for tt in range(TT):
                    last = nc.gpsimd.memset(v_columns(VA[s][:, tt, :], DH, 1), 1.0)
            last.then_inc(prep_gpsimd, 1)
            with pool.Fori(0, PAIRS) as it:
                for step in STEPS:
                    kind, s = step[0], step[1]
                    if kind == "kx":
                        landed(pool, it, step)
                        nc.gpsimd.tensor_tensor(KT[s][0:ROWS, :, :].rearrange("p g (j n) -> p (g j) n", j=J),
                                                KM[s][0:ROWS, :, :, TAIL_AT:S].rearrange("p g j n -> p (g j) n")
                                                .bitcast(F32),
                                                zeros[0:ROWS, :].rearrange("p (a n) -> p a n", n=TAIL), ALU.add)\
                          .then_inc(sems["tail"], 1)
                    if kind == "y":
                        done(pool, it, f"var{s}", step)
                        nc.gpsimd.tensor_tensor(RST[s][:, :], VE[s][:, :], halves[:, :], ALU.pow)\
                          .then_inc(sems[f"rstd{s}"], 1)
                    if kind == "ln":
                        layer = step[2]
                        if layer in BIAS_AFTER:
                            done(pool, it, f"x{s}", step)
                            nc.gpsimd.tensor_tensor(XB[s][:, :, :], X[s][:, :, :],
                                                    spread(out_bias(BIAS_AFTER[layer]), TT), ALU.add)\
                              .then_inc(sems[f"xb{s}"], 1)

        @block.scalar
        def _(act):
            for name in ("act_freed", "probs", "heads_out"):
                act.sem_inc(sems[name], 1)
            for s in range(NS):
                act.sem_inc(stored[s], 1)
            act.wait_ge(weights_in, 16 * NW)
            with act.Fori(0, PAIRS) as it:
                for step in STEPS:
                    kind, s = step[0], step[1]
                    bank = BANK[BANK_OF[step]] if step in BANK_OF else None
                    if kind == "load":
                        earlier(act, it, f"x{s}")
                        act.wait_ge(stored[s], it * 16 + 1)
                        act.dma_start(X[s][:, :, :], x[bass.ds(it * NS + s, 1), :, :].rearrange(
                            "b (t p) d -> p (b t) d", p=P)).then_inc(x_in[s], 16)
                        act.dma_start(CT[s][:, :], ctxT[bass.ds(it * NS + s, 1), :, :].rearrange(
                            "b p n -> p (b n)")).then_inc(x_in[s], 16)
                    if kind == "store":
                        done(act, it, f"x{s}", ("ln", s, FFN1))
                        act.dma_start(out[bass.ds(it * NS + s, 1), :, :].rearrange("b (t p) d -> p (b t) d", p=P),
                                     X[s][:, :, :]).then_inc(stored[s], 16)
                    if kind == "xt":
                        done(act, it, "bank_full", step)
                        nc.scalar.activation(XT[s][:, :], bank[:, :], ACT.Copy).then_inc(sems["act_freed"], 1)
                    if kind == "turn":
                        done(act, it, "bank_full", step)
                        nc.scalar.activation(OC[s][:, :], bank[:, :], ACT.Copy).then_inc(sems["act_freed"], 1)
                    if kind in ("q", "k", "ktok") and step[2] == LIN:
                        done(act, it, "clipped", step)
                        nc.scalar.activation(T2[s], T1[s], ACT.Exp).then_inc(sems["exped"], 1)
                        if kind != "ktok":
                            done(act, it, "dve_freed", step)
                            nc.scalar.activation((HI if kind == "q" else KHI)[s][:, :],
                                                 (QF if kind == "q" else KF)[s], ACT.Copy)\
                              .then_inc(sems["hi"], 1)
                    elif kind in ("q", "k", "kx"):
                        n = S if kind == "kx" else T
                        done(act, it, "bank_full", step)
                        if step in K_LAST:
                            landed(act, it, K_LAST[step])
                        nc.scalar.activation(SPLITS[kind][0][s][:, 0:n], bank[:, 0:n], ACT.Identity,
                                             bias=qk_bias(step[2], 0 if kind == "q" else 1)).then_inc(sems["hi"], 1)
                    if kind == "shift":
                        done(act, it, "bank_full", step)
                        nc.scalar.activation(QS[s][ROWS:P, step[3], :], bank[ROWS:P, :], ACT.Copy)\
                          .then_inc(sems["act_freed"], 1)
                    if kind == "scores":
                        _, _, layer, g, kt, half = step
                        place = SCORE_PLACE[step]
                        unit = UNIT_AT[("values", s, layer, g, kt)]
                        done(act, it, "scores_full", step)
                        if unit >= 2:
                            done(act, it, "values_done", UNITS[unit - 2])
                        nc.scalar.activation(PR[:, unit % 2, 2 * half:2 * half + 2, :], SC[place][:, :, :], ACT.Exp,
                                             scale=SCALE).then_inc(sems["probs"], 1)
                    if kind == "xscores":
                        _, _, layer, g, part = step
                        place = SCORE_PLACE[step]
                        unit = UNIT_AT[("xvalues", s, layer, g)]
                        done(act, it, "scores_full", step)
                        if unit >= 2:
                            done(act, it, "values_done", UNITS[unit - 2])
                        if part < 2:
                            nc.scalar.activation(PR[:, unit % 2, 2 * part:2 * part + 2, :], SC[place][:, :, :],
                                                 ACT.Exp, scale=SCALE).then_inc(sems["probs"], 1)
                        else:
                            nc.scalar.activation(PT[:, unit % 2, :], SC[place][:, 0, :], ACT.Exp,
                                                 scale=SCALE).then_inc(sems["probs"], 1)
                    if ("heads_out", step) in signals(step):
                        done(act, it, "values_done", step)
                        if step[2] == LIN:
                            nc.scalar.activation(OT[s][:, step[3] % 2, :], OTP[:, :], ACT.Identity, bias=table["eps"])\
                              .then_inc(sems["heads_out"], 1)
                        else:
                            nc.scalar.activation(OT[s][:, step[3] % 2, :], OTP[:, :], ACT.Copy)\
                              .then_inc(sems["heads_out"], 1)
            for s in range(NS):
                act.wait_ge(stored[s], PAIRS * 16 + 1)

        @block.vector
        def _(dve):
            for name in ("dve_freed", "masked", "x0", "x1"):
                dve.sem_inc(sems[name], 1)
            dve.wait_ge(weights_in, 16 * NW)
            nc.vector.tensor_scalar(GT[:, 0, :], WF0[:, :], 0.0, 2.0, ALU.is_ge, ALU.mult).then_inc(prep_vector, 1)
            dve.wait_ge(prep_vector, 1)
            nc.vector.scalar_tensor_tensor(WF0[:, :], GT[:, 0, :], -1.0, F0R[:, 0, :], ALU.add, ALU.mult)\
              .then_inc(prep_vector, 1)
            dve.wait_ge(prep_vector, 2)
            dve.wait_ge(prep_tensor, 1)
            nc.vector.tensor_copy(GT[:, :, :], BANK[0][:, 0:2 * D].rearrange("p (a d) -> p a d", a=2))\
              .then_inc(prep_vector, 1)
            dve.wait_ge(prep_tensor, 2)
            nc.vector.tensor_scalar(WF1[:, :], BANK[0][:, 0:D], 1.0 / D, None, ALU.mult).then_inc(prep_vector, 1)
            nc.vector.tensor_copy(identr[:, :], ident).then_inc(prep_vector, 1)
            for i in range(2):
                nc.vector.tensor_scalar(BVM[:, i, :], BXR[i][:, 0, :], table["tailmask"], None, ALU.mult)\
                  .then_inc(prep_vector, 1)
            dve.wait_ge(prep_gpsimd, N_GPREP)
            for j in range(J):
                aug = table["augmask"][ROWS:P, j:j + 1]
                nc.vector.tensor_scalar(PR[ROWS:P, 0, j, :], zeros[ROWS:P, :], aug, None, ALU.add)\
                  .then_inc(prep_vector, 1)
                for s in range(NS):
                    nc.vector.tensor_scalar(KT[s][ROWS:P, :, j * TAIL:j * TAIL + TAIL],
                                            zeros[ROWS:P, 0:G * TAIL].rearrange("p (g n) -> p g n", g=G), aug, None,
                                            ALU.add).then_inc(prep_vector, 1)
                    r = slice(VW * j, VW * j + VW)
                    for up in range(2):
                        nc.vector.tensor_scalar(
                            VT[s][r, up * G // 2:(up + 1) * G // 2, VW * j + up * HALF + DH], zeros[r, 0:G // 2],
                            table["tailmask"][r, :], None, ALU.add).then_inc(prep_vector, 1)
            dve.wait_ge(prep_vector, N_VPREP)
            dve.wait_ge(aug_in, 16 * NS * G)
            with dve.Fori(0, PAIRS) as it:
                chain = [0]
                CH = DVE_CHAIN

                def link(ins):
                    chain[0] += 1
                    ins.then_inc(dve_self, 1)
                    dve.wait_ge(dve_self, it * CH + chain[0])

                for step in STEPS:
                    kind, s = step[0], step[1]
                    bank = BANK[BANK_OF[step]] if step in BANK_OF else None
                    if kind in ("q", "k", "ktok") and step[2] == LIN:
                        done(dve, it, "bank_full", step)
                        nc.vector.tensor_scalar(T1[s], bank[:, :], 0.0, None, ALU.min).then_inc(sems["clipped"], 1)
                        done(dve, it, "exped", step)
                        dst = {"q": QF[s], "k": KF[s], "ktok": OT[s][:, 1, :]}[kind]
                        nc.vector.scalar_tensor_tensor(dst, bank[:, :], 0.0, T2[s], ALU.max, ALU.add)\
                          .then_inc(sems["dve_freed"], 1)
                        if kind != "ktok":
                            done(dve, it, "hi", step)
                            done(dve, it, "dve_freed", step)
                            nc.vector.tensor_tensor((LO if kind == "q" else KLO)[s][:, :], dst,
                                                    (HI if kind == "q" else KHI)[s][:, :].bitcast(F32), ALU.subtract)\
                              .then_inc(sems["lo"], 1)
                    elif kind in ("q", "k", "kx"):
                        n = S if kind == "kx" else T
                        hi, lo = [part[s] for part in SPLITS[kind]]
                        done(dve, it, "hi", step)
                        nc.vector.scalar_tensor_tensor(lo[:, 0:n], bank[:, 0:n],
                                                       qk_bias(step[2], 0 if kind == "q" else 1),
                                                       hi[:, 0:n].bitcast(F32), ALU.add, ALU.subtract)\
                          .then_inc(sems["dve_freed"], 1)
                    if kind == "v":
                        done(dve, it, "bank_full", step)
                        for tt in range(TT):
                            dst = v_columns(VA[s][:, tt, :], 0, DH)
                            src = bank[:, tt * D:tt * D + D].rearrange("p (u h c) -> p u h c", u=2, c=DH)
                            if step[2] == LIN:
                                ins = nc.vector.tensor_copy(dst, src)
                            else:
                                vb = v_bias(step[2]).rearrange("p (u h c) -> p u h c", u=2, c=DH)
                                ins = nc.vector.tensor_tensor(dst, src, vb, ALU.add)
                        ins.then_inc(sems["dve_freed"], 1)
                    if kind == "vx":
                        i = 0 if step[2] == X0 else 1
                        done(dve, it, "bank_full", step)
                        vb = v_bias(step[2]).rearrange("p (u h c) -> p u h c", u=2, c=DH)
                        nc.vector.tensor_tensor(v_columns(VA[s][:, 0, :], 0, DH),
                                                bank[:, 0:D].rearrange("p (u h c) -> p u h c", u=2, c=DH), vb,
                                                ALU.add)
                        tail = bank[:, D:2 * D].rearrange("p (g j c) -> p g j c", g=G, j=J)
                        vb = BVM[:, i, :].rearrange("p (g j c) -> p g j c", g=G, j=J)
                        for j in range(J):
                            r = slice(VW * j, VW * j + VW)
                            for up in range(2):
                                g = slice(up * G // 2, (up + 1) * G // 2)
                                c = VW * j + up * HALF
                                ins = nc.vector.scalar_tensor_tensor(VT[s][r, g, c:c + DH], tail[r, g, j, :],
                                                                     table["tailmask"][r, :], vb[r, g, j, :],
                                                                     ALU.mult, ALU.add)
                        ins.then_inc(sems["dve_freed"], 1)
                    if kind == "state":
                        done(dve, it, "bank_full", step)
                        if step[3] == 0:
                            landed(dve, it, ("q", s, LIN))
                        nc.vector.tensor_tensor(SM[s][:, step[3], :], bank[:, :], table["blockdiag"], ALU.mult)\
                          .then_inc(sems["dve_freed"], 1)
                    if kind == "lin_scores":
                        _, _, layer, g, p = step
                        place = SCORE_PLACE[step]
                        unit = UNIT_AT[("lin_values", s, layer, g, p)]
                        done(dve, it, "scores_full", step)
                        if unit >= 2:
                            done(dve, it, "values_done", UNITS[unit - 2])
                        for c in range(2):
                            ins = nc.vector.tensor_tensor(
                                PR[:, unit % 2, c, :].rearrange("p (j t) -> p j t", j=J),
                                SC[place][:, c, :].rearrange("p (j t) -> p j t", j=J),
                                spread(table["causal"], J), ALU.mult)
                        ins.then_inc(sems["masked"], 1)
                    if kind == "max":
                        _, _, layer, g, qt, j = step
                        done(dve, it, "bank_full", step)
                        if layer == SELF:
                            src, dst = bank[:, :], NEG[s][:, g, qt, j:j + 1]
                        else:
                            src = bank[:, 0:2 * S].rearrange("p (a n) -> p a n", a=2)
                            dst = NEG[s][:, g, qt, 2 * j:2 * j + 2]
                        nc.vector.tensor_reduce(dst, src, AX.X, ALU.max, negate=True).then_inc(sems["dve_freed"], 1)
                    if kind == "split":
                        _, _, layer, g = step
                        place = GROUPS.index(g)
                        done(dve, it, "dve_freed", [x for x in STEPS if x[0:4] == ("max", s, layer, g)][-1])
                        if place >= 2:
                            done(dve, it, "act_freed", ("shift", s, layer, GROUPS[place - 2]))
                        nmp = NMP[s][place % 2]
                        hi = nmp[:, :, ROWS:ROWS + J]
                        link(nc.vector.tensor_copy(hi, NEG[s][:, g, :, :]))
                        nc.vector.tensor_tensor(nmp[:, :, ROWS + J:ROWS + 2 * J], NEG[s][:, g, :, :],
                                                hi.bitcast(F32), ALU.subtract).then_inc(sems["shift_split"], 1)
                    if kind == "norm":
                        b = step[3]
                        done(dve, it, "bank_full", step)
                        m = bank[:, :].rearrange("p (t j u c) -> p t j u c", t=TT, j=J, u=2)
                        den = bank[:, :].rearrange("p (n c) -> p n c", c=HALF)[:, :, DH]
                        link(nc.vector.reciprocal(REC[s][:, b, :], den))
                        o = O[s][:, :, :].rearrange("p t (u b j c) -> p t u b j c", u=2, b=2, j=J)
                        for u in range(2):
                            r = REC[s][:, b, u:u + 1]
                            rb = bass.AP(tensor=r.tensor, offset=r.offset,
                                         ap=[list(r.ap[0]), [2 * J, TT], [2, J], [0, DH]])
                            ins = nc.vector.tensor_tensor(o[:, :, u, b, :, :], m[:, :, :, u, 0:DH], rb, ALU.mult)
                        ins.then_inc(sems["dve_freed"], 1)
                    if kind == "y":
                        layer = step[2]
                        z = Z[s][:, :, :]
                        y = bank[:, :].rearrange("p (t d) -> p t d", t=TT)
                        done(dve, it, "bank_full", step)
                        if layer == FFN0:
                            for tt in range(TT):
                                ins = nc.vector.tensor_tensor(Z[s][:, tt, :], y[:, tt, :], F0R[:, 1, :], ALU.add)
                            ins.then_inc(sems["dve_freed"], 1)
                            done(dve, it, "dve_freed", step)
                            link(nc.vector.tensor_scalar(z, z, MAX_VAL, -MAX_VAL, ALU.min, ALU.max))
                            link(nc.vector.tensor_tensor(z, z, X[s][:, :, :], ALU.add))
                        else:
                            res = X[s] if layer == LIN else XB[s]
                            if layer != LIN:
                                done(dve, it, f"xb{s}", ("ln", s, layer - 1))
                            nc.vector.tensor_tensor(z, y, res[:, :, :], ALU.add).then_inc(sems["dve_freed"], 1)
                            done(dve, it, "dve_freed", step)
                        for tt in range(TT):
                            ins = nc.vector.bn_stats(ST6[s][:, tt, :], Z[s][:, tt, :])
                        link(ins)
                        nc.vector.memset(MARK[:, :], 0.0)
                        for tt in range(TT):
                            ins = nc.vector.bn_aggr(MV[s][:, tt, :], ST6[s][:, tt, :])
                        link(ins)
                        nc.vector.tensor_scalar(VE[s][:, :], MV[s][:, :, 1], EPS_LN, None, ALU.add)\
                          .then_inc(sems[f"var{s}"], 1)
                    if kind == "ln":
                        done(dve, it, f"rstd{s}", ("y", s, step[2]))
                        for tt in range(TT):
                            ins = nc.vector.tensor_scalar(X[s][:, tt, :], Z[s][:, tt, :], MV[s][:, tt, 0:1],
                                                          RST[s][:, tt:tt + 1], ALU.subtract, ALU.mult)
                        ins.then_inc(sems[f"x{s}"], 1)
                assert chain[0] == CH, chain[0]

        @block.tensor
        def _(pe):
            mm = nc.tensor.matmul
            pe.wait_ge(weights_in, 16 * NW)
            mm(BANK[0][:, 0:D], WFR[:, 0, :], table["cos"], start=True, stop=False)
            mm(BANK[0][:, 0:D], WFR[:, 1, :], table["sin"], start=False, stop=True)
            mm(BANK[0][:, D:2 * D], WFR[:, 1, :], table["cos"], start=True, stop=False)
            mm(BANK[0][:, D:2 * D], WFR[:, 0, :], table["nsin"], start=False, stop=True).then_inc(prep_tensor, 1)
            pe.wait_ge(prep_vector, 3)
            mm(BANK[0][:, 0:D], GT[:, 0, :], table["cos"], start=True, stop=False)
            mm(BANK[0][:, 0:D], GT[:, 1, :], table["nsin"], start=False, stop=True).then_inc(prep_tensor, 1)
            pe.wait_ge(prep_vector, 4)
            pe.wait_ge(prep_gpsimd, N_GPREP)
            pe.wait_ge(prep_vector, N_VPREP)
            pe.wait_ge(aug_in, 16 * NS * G)
            with pe.Fori(0, PAIRS) as it:
                for step in STEPS:
                    kind, s = step[0], step[1]
                    bank = BANK[BANK_OF[step]] if step in BANK_OF else None
                    if kind == "xt":
                        if step[2] == LIN:
                            pe.wait_ge(x_in[s], it * 32 + 32)
                        else:
                            done(pe, it, f"x{s}", x_key(s, step[2]))
                        ready(pe, it, step)
                        for tt in range(TT):
                            ins = nc.tensor.transpose(bank[:, tt * P:tt * P + P], X[s][:, tt, :], ident)
                        ins.then_inc(sems["bank_full"], 1)
                    if kind in ("q", "k"):
                        ready(pe, it, step, ("xt", s, step[2]))
                        mm(bank[:, :], (w_q if kind == "q" else w_k)(step[2]), XT[s][:, :], start=True, stop=True)\
                            .then_inc(sems["bank_full"], 1)
                    if kind == "kx":
                        ready(pe, it, step)
                        pe.wait_ge(x_in[s], it * 32 + 32)
                        mm(bank[:, 0:S], w_k(step[2]), CT[s][:, :], start=True, stop=True)\
                            .then_inc(sems["bank_full"], 1)
                    if kind == "vx":
                        ready(pe, it, step)
                        mm(bank[:, 0:D], CT[s][:, 0:P], w_v(step[2]), start=True, stop=True)
                        for j in range(J):
                            ins = mm(bank[VW * j:VW * j + VW, D:2 * D], CT[s][:, TAIL_AT:S], w_v(step[2]),
                                     start=True, stop=True)
                        ins.then_inc(sems["bank_full"], 1)
                    if kind in ("v", "ktok"):
                        ready(pe, it, step, ("xt", s, step[2]))
                        w = w_v(step[2]) if kind == "v" else w_k(step[2])
                        for tt in range(TT):
                            ins = mm(bank[:, tt * D:tt * D + D], XT[s][:, tt * P:tt * P + P], w, start=True, stop=True)
                        ins.then_inc(sems["bank_full"], 1)
                    if kind == "state":
                        c = step[3]
                        ready(pe, it, step, ("v", s, LIN), ("ktok", s, LIN))
                        mm(bank[:, :], KTOK[s][:, c, :], VA[s][:, c, :], start=(c == 0), stop=True,
                           skip_group_check=True).then_inc(sems["bank_full"], 1)
                    if kind == "lin_scores":
                        _, _, layer, g, p = step
                        if p == 0:
                            if g == 0:
                                landed(pe, it, ("q", s, layer))
                                landed(pe, it, ("k", s, layer))
                        score_empty(pe, it, step)
                        place = SCORE_PLACE[step]
                        for c in range(2):
                            t = slice((2 * p + c) * P, (2 * p + c + 1) * P)
                            for j in range(J):
                                ins = mm(SC[place][:, c, j * P:j * P + P], KM[s][0:ROWS, g, j, t], QS[s][0:ROWS, g, t],
                                         start=True, stop=True)
                        ins.then_inc(sems["scores_full"], 1)
                    if kind == "lin_values":
                        _, _, layer, g, p = step
                        unit = UNIT_AT[step]
                        done(pe, it, "masked", ("lin_scores", s, layer, g, p))
                        if p == 0:
                            if g < G // 2:
                                heads_out_free(pe, it, step)
                            if g == 0:
                                done(pe, it, "dve_freed", ("state", s, layer, TT - 2))
                        for c in range(2):
                            n = 2 * p + c
                            t = slice(n * P, n * P + P)
                            if n:
                                mm(OTP[:, t], SM[s][:, n - 1, g * P:g * P + P], QF[s][:, t], start=False,
                                   stop=False, skip_group_check=True)
                            for j in range(J):
                                h = g * J + j
                                ins = mm(OTP[VW * j:VW * j + VW, t], VA[s][:, n, h * VW:h * VW + VW],
                                         PR[:, unit % 2, c, j * P:j * P + P], start=(n == 0 and g < G // 2), stop=True,
                                         skip_group_check=True)
                        ins.then_inc(sems["values_done"], 1)
                    if kind == "max":
                        _, _, layer, g, qt, j = step
                        if qt == 0 and j == 0:
                            if g == 0:
                                landed(pe, it, ("q", s, layer))
                                landed(pe, it, ("k" if layer == SELF else "kx", s, layer))
                        ready(pe, it, step)
                        q = QS[s][0:ROWS, g, qt * P:qt * P + P]
                        if layer == SELF:
                            ins = mm(bank[:, :], q, KM[s][0:ROWS, g, j, :], start=True, stop=True)
                        else:
                            ins = mm(bank[:, 0:2 * S].rearrange("p (a n) -> p a n", a=2), q,
                                     KM[s][0:ROWS, g, 2 * j:2 * j + 2, 0:S], start=True, stop=True)
                        ins.then_inc(sems["bank_full"], 1)
                    if kind == "shift":
                        done(pe, it, "shift_split", ("split", *step[1:]))
                        ready(pe, it, step)
                        for qt in range(TT):
                            ins = mm(bank[:, qt * P:qt * P + P], NMP[s][GROUPS.index(step[3]) % 2][:, qt, :],
                                     identr[:, :], start=True, stop=True)
                        ins.then_inc(sems["bank_full"], 1)
                    if kind == "scores":
                        _, _, layer, g, kt, half = step
                        if kt == 0 and half == 0:
                            done(pe, it, "act_freed", ("shift", s, layer, g))
                        score_empty(pe, it, step)
                        place = SCORE_PLACE[step]
                        for a in range(2):
                            ins = mm(SC[place][:, a, :], KM[s][:, g, 2 * half + a, kt * P:kt * P + P], QS[s][:, g, :],
                                     start=True, stop=True)
                        ins.then_inc(sems["scores_full"], 1)
                    if kind == "values":
                        _, _, layer, g, kt = step
                        unit = UNIT_AT[step]
                        done(pe, it, "probs", ("scores", s, layer, g, kt, 1))
                        if kt == 0:
                            if g < G // 2:
                                heads_out_free(pe, it, step)
                            if g == 0:
                                done(pe, it, "dve_freed", ("v", s, layer))
                        for j in range(J):
                            h = g * J + j
                            ins = mm(OTP[VW * j:VW * j + VW, :], VA[s][:, kt, h * VW:h * VW + VW],
                                     PR[:, unit % 2, j, :], start=(kt == 0 and g < G // 2),
                                     stop=(kt == TT - 1 and g >= G // 2))
                        ins.then_inc(sems["values_done"], 1)
                    if kind == "xscores":
                        _, _, layer, g, part = step
                        if part == 0:
                            done(pe, it, "act_freed", ("shift", s, layer, g))
                            if g == 0:
                                done(pe, it, "tail", ("kx", s, layer))
                        score_empty(pe, it, step)
                        place = SCORE_PLACE[step]
                        if part < 2:
                            for a in range(2):
                                ins = mm(SC[place][:, a, :], KM[s][:, g, 2 * part + a, 0:P], QS[s][:, g, :],
                                         start=True, stop=True)
                        else:
                            ins = mm(SC[place][:, 0, :], KT[s][:, g, :], QS[s][:, g, :], start=True, stop=True)
                        ins.then_inc(sems["scores_full"], 1)
                    if kind == "xvalues":
                        _, _, layer, g = step
                        unit = UNIT_AT[step]
                        done(pe, it, "probs", ("xscores", s, layer, g, 2))
                        if g < G // 2:
                            heads_out_free(pe, it, step)
                        if g == 0:
                            done(pe, it, "dve_freed", ("vx", s, layer))
                        mm(OTP[:, :], VT[s][:, g, :], PT[:, unit % 2, :], start=(g < G // 2), stop=False,
                           skip_group_check=True)
                        for j in range(J):
                            h = g * J + j
                            ins = mm(OTP[VW * j:VW * j + VW, :], VA[s][:, 0, h * VW:h * VW + VW], PR[:, unit % 2, j, :],
                                     start=False, stop=True, skip_group_check=True)
                        ins.then_inc(sems["values_done"], 1)
                    if kind == "norm":
                        _, _, layer, b = step
                        ready(pe, it, step)
                        done(pe, it, "heads_out", bank_end(s, layer, b))
                        for tt in range(TT):
                            ins = nc.tensor.transpose(bank[:, tt * P:tt * P + P], OT[s][:, b, tt * P:tt * P + P], ident)
                        ins.then_inc(sems["bank_full"], 1)
                    if kind == "turn":
                        ready(pe, it, step, *[("norm", s, step[2], b) for b in range(G // 2)])
                        for tt in range(TT):
                            ins = nc.tensor.transpose(bank[:, tt * P:tt * P + P], O[s][:, tt, :], ident)
                        ins.then_inc(sems["bank_full"], 1)
                    if kind == "y":
                        layer = step[2]
                        ready(pe, it, step, ("xt" if layer in (FFN0, FFN1) else "turn", s, layer))
                        src = XT[s] if layer in (FFN0, FFN1) else OC[s]
                        for tt in range(TT):
                            ins = mm(bank[:, tt * D:tt * D + D], src[:, tt * P:tt * P + P], w_out(layer),
                                     start=True, stop=True)
                        ins.then_inc(sems["bank_full"], 1)


def kernel(**inputs):
    import numpy as _np
    import concourse.bacc as _bacc
    from concourse import mybir as _mybir
    from concourse.bass_utils import run_bass_kernel_spmd as _run

    a = {k: _np.asarray(v) for k, v in inputs.items()}
    cross = lambda pre, q, k, v, o: _np.stack([a[pre + n].T for n in (q, k, v, o)], axis=1)
    arrays = {
        "x": a["x"],
        "ctxT": a["ctx_1024"].transpose(0, 2, 1),
        "w_lin": a["L0_attn_w_attn"],
        "w_lin_proj": a["L0_attn_w_proj"],
        "wx0": cross("L0_xattn_W", "q", "k", "v", "o"),
        "bx0": _np.stack([a["L0_xattn_bq"], a["L0_xattn_bk"]], axis=1),
        "bx0_row": _np.stack([a["L0_xattn_bv"], a["L0_xattn_bo"]]),
        "w_ffn0": a["L0_ffn_weights"].T,
        "ffn0_row": _np.stack([a["L0_ffn_scale"], a["L0_ffn_bias"]]),
        "w_self": a["L1_attn_w_qkv"],
        "b_self": a["L1_attn_b_qkv"].reshape(3, D)[0:2].T,
        "b_self_row": _np.stack([a["L1_attn_b_qkv"][2 * D:], a["L1_attn_b_out"]]),
        "w_self_out": a["L1_attn_w_out"],
        "wx1": cross("L1_xattn_w_", "q", "k", "v", "o"),
        "bx1": _np.stack([a["L1_xattn_b_q"], a["L1_xattn_b_k"]], axis=1),
        "bx1_row": _np.stack([a["L1_xattn_b_v"], a["L1_xattn_b_o"]]),
        "w_freq": _np.stack([a["L1_ffn_w_freq_real"], a["L1_ffn_w_freq_imag"]], axis=1),
        "ffn1_row": a["L1_ffn_bias"],
        "const": CONST,
    }
    arrays = {f"in_{k}_dram": _np.ascontiguousarray(v) for k, v in arrays.items()}
    nc = _bacc.Bacc("TRN2", target_bir_lowering=False, num_devices=1)
    args = [nc.dram_tensor(k, v.shape, _mybir.dt.from_np(v.dtype), kind="ExternalInput").ap()
            for k, v in arrays.items()]
    args.append(nc.dram_tensor("out_0_dram", (B, T, D), _mybir.dt.from_np(_np.dtype("float32")),
                               kind="ExternalOutput").ap())
    build(nc, *args)
    r = _run(nc, [arrays], core_ids=[0])
    return r.results[0]["out_0_dram"]
```

```python
from contextlib import ExitStack

import numpy as np

import concourse.bass as bass
from concourse import mybir

F32 = mybir.dt.float32
F32R = mybir.dt.float32r
ACT = mybir.ActivationFunctionType
ALU = mybir.AluOpType
AX = mybir.AxisListType

P = 128
B, T, D = 4, 512, 128
S = 154
H, DH = 16, 8
G, J = 4, 4
TT = T // P
SPLIT = 32
ROWS = 3 * SPLIT
VW = 32
HALF = VW // 2
GROUPS = (0, 2, 1, 3)
TAIL = 32
TAIL_AT = S - TAIL
NS = 2
PAIRS = B // NS
SCALE = float(DH) ** -0.5
EPS_LN = 1e-5
EPS_DEN = 1e-6
MAX_VAL = 100.0

LIN, X0, FFN0, SELF, X1, FFN1 = range(6)
ATTN = (LIN, X0, SELF, X1)


def constants():
    r = np.arange(P)
    k = 2 * np.pi * ((r[:, None] * r[None, :]) % D) / D
    parts = {
        "ident": np.eye(P),
        "cos": np.cos(k),
        "sin": np.sin(k),
        "nsin": -np.sin(k),
        "causal": (r[:, None] <= r[None, :]),
        "headmask": (r[:, None] % SPLIT // DH == np.arange(J)[None, :]),
        "augmask": (r[:, None] >= ROWS) & (r[:, None] < ROWS + 2 * J) & (r[:, None] % J == np.arange(J)[None, :]),
        "tailmask": (r[:, None] % TAIL >= P - TAIL_AT),
        "eps": EPS_DEN * (r[:, None] % HALF == DH),
        "blockdiag": (r[:, None] // DH == np.arange(H * VW)[None, :] // VW),
    }
    at, out = {}, []
    n = 0
    for name, a in parts.items():
        at[name] = (n, n + a.shape[1])
        n += a.shape[1]
        out.append(a.astype(np.float32))
    return at, np.ascontiguousarray(np.concatenate(out, axis=1))


CONST_AT, CONST = constants()


def attention_steps(s, layer):
    shifts, scores, values = [], [], []
    for place, g in enumerate(GROUPS):
        if layer == LIN:
            scores += [("lin_scores", s, layer, g, p) for p in range(2)]
            values += [("lin_values", s, layer, g, p) for p in range(2)]
            continue
        shifts += [("max", s, layer, g, qt, j) for j in range(J if layer == SELF else 2) for qt in range(TT)]
        shifts += [("split", s, layer, g), ("shift", s, layer, g)]
        if layer == SELF:
            scores += [("scores", s, layer, g, kt, half) for kt in range(TT) for half in range(2)]
            values += [("values", s, layer, g, kt) for kt in range(TT)]
        else:
            scores += [("xscores", s, layer, g, part) for part in range(3)]
            values += [("xvalues", s, layer, g)]
    return shifts, scores, values


def unit_of(step):
    kind, s, layer, g = step[:4]
    return {"scores": ("values", s, layer, g, step[4]), "xscores": ("xvalues", s, layer, g),
            "lin_scores": ("lin_values", s, layer, g, step[4])}[kind]


def needs(step):
    kind, s = step[:2]
    if kind == "load":
        return []
    layer = step[2] if kind != "store" else FFN1
    q, k, v = [(n, s, layer) for n in (("q", "kx", "vx") if layer in (X0, X1) else ("q", "k", "v"))]
    if kind == "xt":
        return [("load", s) if layer == LIN else ("ln", s, layer - 1)]
    if kind == "kx":
        return [attention_steps(s, layer - 1)[1][-1]]
    if kind == "vx":
        return [attention_steps(s, layer - 1)[2][-1]]
    if kind in ("q", "k", "v", "ktok"):
        return [("xt", s, layer)]
    if kind == "state":
        return [v, q, ("ktok", s, layer)] + ([("state", s, layer, step[3] - 1)] if step[3] else [])
    if kind == "lin_scores":
        return [q, k]
    if kind == "max":
        return [(*q, step[3]), k]
    if kind == "split":
        g = step[3]
        place = GROUPS.index(g)
        return [("max", s, layer, g, TT - 1, J - 1 if layer == SELF else 1)] + \
               ([("shift", s, layer, GROUPS[place - 2])] if place >= 2 else [])
    if kind == "shift":
        return [("split", s, layer, step[3])]
    if kind in ("scores", "xscores"):
        return [("shift", s, layer, step[3]), k]
    if kind == "values":
        return [("scores", *step[1:], 1), v]
    if kind == "xvalues":
        return [("xscores", *step[1:], 2), v]
    if kind == "lin_values":
        return [("lin_scores", *step[1:]), ("state", s, layer, TT - 2)]
    if kind == "norm":
        last = G // 2 + step[3]
        return [("xvalues", s, layer, last) if layer in (X0, X1) else
                ("values", s, layer, last, TT - 1) if layer == SELF else ("lin_values", s, layer, last, 1)]
    if kind == "y":
        return [("xt" if layer in (FFN0, FFN1) else "turn", s, layer)]
    if kind == "turn":
        return [("norm", s, layer, b) for b in range(G // 2)]
    if kind in ("ln", "store"):
        return [("y" if kind == "ln" else "ln", s, layer)]
    raise ValueError(kind)


def stages(step):
    kind = step[0]
    layer = step[2] if len(step) > 2 else None
    if kind == "load":
        return [("queue", 2.5)], 0
    if kind == "store":
        return [("queue", 2.0)], 0
    if kind in ("xt", "turn"):
        return [("pe", .6), ("act", .5)], 1
    if kind in ("q", "k"):
        dma = ("dma", 5.8 if kind == "q" else 9.8)
        if layer == LIN:
            return [("pe", .7), ("dve", .6), ("act", .52), ("dve", .6), ("act", .52), ("dve", .6), dma], 3
        return [("pe", .7), ("act", .48), ("dve", .54)] + ([dma] if kind == "k" else []), 2
    if kind == "kx":
        return [("pe", .2), ("act", .3), ("dve", .25), ("dma", 9.), ("pool", 1.)], 2
    if kind == "ktok":
        return [("pe", .7), ("dve", .6), ("act", .52), ("dve", .6)], 3
    if kind == "v":
        return [("pe", .7), ("dve", .8)], 1
    if kind == "vx":
        return [("pe", .5), ("dve", 1.4)], 1
    if kind == "state":
        return [("pe", .7), ("dve", .6)], 1
    if kind == "max":
        return ([("pe", .24), ("dve", .59)] if layer == SELF else [("pe", .18), ("dve", .39)]), 1
    if kind == "split":
        return [("dve", .35)], 0
    if kind == "shift":
        return [("pe", .28), ("act", .48)], 1
    if kind in ("scores", "xscores"):
        return ([("pe", .24), ("act", .48)] if kind == "xscores" and step[4] == 2 else
                [("pe", .48), ("act", .9)]), 1
    if kind == "lin_scores":
        return [("pe", .62), ("dve", 1.2)], 1
    if kind in VALUES_KINDS:
        pe = {"values": .95, "xvalues": 1.8, "lin_values": 1.2}[kind]
        return ([("pe", pe), ("act", .48)] if ("heads_out", step) in signals(step) else [("pe", pe)]), 0
    if kind == "norm":
        return [("pe", .55), ("dve", .75)], 1
    if kind == "y":
        return [("pe", .6 if layer == FFN1 else .8), ("dve", 2.), ("pool", 1.)], 1
    if kind == "ln":
        return [("dve", 1.)] + ([("pool", 1.2)] if layer in BIAS_AFTER else []), 0
    raise ValueError(kind)


def plan():
    sequences = []
    for s in range(NS):
        chain = [("load", s)]
        for layer in ATTN:
            names = {LIN: ("xt", "k", "q", "v", "ktok"), SELF: ("xt", "k")}.get(layer, ("xt",))
            chain += [(n, s, layer) for n in names]
            if layer != LIN:
                chain += [("q", s, layer, g) for g in GROUPS[0:1]]
                chain += [("v", s, layer)] if layer == SELF else []
                chain += [("q", s, layer, g) for g in GROUPS[1:]]
            else:
                chain += [("state", s, layer, c) for c in range(TT - 1)]
            chain += [("norm", s, layer, b) for b in range(G // 2)] + \
                     [("turn", s, layer), ("y", s, layer), ("ln", s, layer)]
            if layer in (X0, X1):
                chain += [("xt", s, layer + 1), ("y", s, layer + 1), ("ln", s, layer + 1)]
        chain.append(("store", s))
        sequences += [chain, [(n, s, layer) for layer in (X0, X1) for n in ("kx", "vx")]]
        parts = [attention_steps(s, layer) for layer in ATTN]
        sequences += [[x for part in parts for x in part[n]] for n in range(3)]
    every = [x for seq in sequences for x in seq]
    users = {x: [] for x in every}
    for x in every:
        for y in needs(x):
            users[y].append(x)
    for seq in sequences:
        if seq[0][0] not in ("load", "kx"):
            for a, b in zip(seq, seq[1:]):
                users[a].append(b)
    way = {}

    def length(x):
        if x not in way:
            way[x] = sum(t for _, t in stages(x)[0]) + max((length(u) for u in users[x]), default=0.0)
        return way[x]

    free = dict.fromkeys(("pe", "act", "dve", "pool", "dma", "queue"), 0.0)
    score_free, heads_free = [0.0, 0.0], 0.0
    bank_free, bank_of = [0.0] * BANKS, {}
    summing = None
    end, opened, units_done = {}, [], 0
    scores_left = {}
    for x in every:
        if x[0] in SCORES_KINDS:
            scores_left[bank_id(x)] = scores_left.get(bank_id(x), 0) + 1
    out = []

    def times(step):
        parts, frees = stages(step)
        t = max((end[x] - (1.35 * (J - 1 - step[5]) if step[0] == "max" and x[0] == "k" else 0.0)
                 for x in needs(step)), default=0.0) + LAG
        bank = None
        if step[0] in SCORES_KINDS:
            t = max(t, score_free[0] + LAG)
        if step[0] in BANK_KINDS:
            if step[0] == "state" and step[3]:
                bank = bank_of["state", step[1], LIN, step[3] - 1]
            else:
                bank = min((b for b in range(BANKS) if b != summing), key=lambda b: bank_free[b])
            t = max(t, bank_free[bank] + LAG)
        if step in HEADS_START:
            t = max(t, heads_free + LAG)
        begun, begin = [], None
        now = dict(free)
        for n, (eng, dur) in enumerate(parts):
            start = max(t, now[eng])
            if n == 0:
                begin = start
            t = start + dur
            now[eng] = t
            begun.append(t)
            t += LAG
        return begin, bank, begun, now, frees

    heads = [list(seq) for seq in sequences]
    while any(heads):
        best = None
        for n, seq in enumerate(heads):
            if not seq:
                continue
            x = seq[0]
            if any(y not in end for y in needs(x)):
                continue
            if x[0] in SCORES_KINDS:
                u = unit_of(x)
                if u not in opened and (len(opened) >= units_done + 2 or (
                        opened and bank_id(opened[-1]) != bank_id(x) and scores_left[bank_id(opened[-1])])):
                    continue
            if x[0] in VALUES_KINDS and opened[units_done] != x:
                continue
            if x[0] == "state" and x[3] == 0 and summing is not None:
                continue
            begin, bank, begun, now, frees = times(x)
            key = begin - LEAD.get(x[0], LEAD["chain"]) - WAY * length(x)
            if best is None or key < best[0]:
                best = (key, n, x, bank, begun, now, frees)
        assert best, [h[0] for h in heads if h]
        _, n, x, bank, begun, now, frees = best
        heads[n].pop(0)
        free.update(now)
        end[x] = begun[0] if x[0] == "ln" else begun[-1]
        if bank is not None:
            bank_free[bank], bank_of[x] = begun[frees], bank
            if x[0] == "state":
                summing = bank if x[3] < TT - 2 else None
        if x[0] in SCORES_KINDS:
            if unit_of(x) not in opened:
                opened.append(unit_of(x))
            scores_left[bank_id(x)] -= 1
            score_free = score_free[1:] + [begun[frees]]
        if x[0] in VALUES_KINDS:
            units_done += 1
            if ("heads_out", x) in signals(x):
                heads_free = begun[-1]
        out.append(x)
    return out, bank_of, max(end.values())


LAG = .2
WAY = .0007
LEAD = {"chain": .12, "max": .16, "split": 7.6, "shift": .43, "scores": .07, "xscores": .1, "lin_scores": 0.,
        "values": .04, "xvalues": 0., "lin_values": .08}
BANKS = 3
BANK_KINDS = ("max", "xt", "q", "k", "kx", "v", "vx", "ktok", "state", "shift", "norm", "turn", "y")
VALUES_KINDS = ("values", "lin_values", "xvalues")
SCORES_KINDS = ("scores", "xscores", "lin_scores")
HEADS_START = {x for s in range(NS) for layer in ATTN for x in attention_steps(s, layer)[2]
               if x[3] < G // 2 and (len(x) == 4 or x[4] == 0)}


def bank_id(step):
    return step[1], step[2], step[3] % 2


BIAS_AFTER = {LIN: X0, FFN0: SELF, SELF: X1, X1: FFN1}


def freed(step):
    return "act_freed" if step[0] in ("xt", "turn", "shift") else "dve_freed"


def signals(step):
    kind, rest = step[0], step[1:]
    s = rest[0]
    if kind in BANK_KINDS:
        out = [("bank_full", step), (freed(step), step)]
        if kind in ("q", "k", "ktok") and rest[1] == LIN:
            out += [("clipped", step), ("exped", step)]
        if kind in ("q", "k", "kx"):
            out.append(("hi", step))
        if kind in ("q", "k") and rest[1] == LIN:
            out.append(("lo", step))
        if kind == "kx":
            out.append(("tail", step))
        if kind == "y":
            out += [(f"var{s}", step), (f"rstd{s}", step)]
        return out
    if kind == "split":
        return [("shift_split", step)]
    if kind in ("scores", "xscores"):
        return [("scores_full", step), ("probs", step)]
    if kind == "lin_scores":
        return [("scores_full", step), ("masked", step)]
    if kind in ("values", "lin_values", "xvalues"):
        out = [("values_done", step)]
        if rest[2] >= G // 2 and (kind == "xvalues" or rest[3] == (TT if kind == "values" else 2) - 1):
            out.append(("heads_out", step))
        return out
    if kind == "ln":
        out = [(f"x{s}", step)]
        if rest[1] in BIAS_AFTER:
            out.append((f"xb{s}", step))
        return out
    return []


STEPS, BANK_OF, _ = plan()


def count():
    value, total = {}, {}
    for step in STEPS:
        for name, key in signals(step):
            total[name] = total.get(name, 0) + 1
            value[name, key] = total[name]
    return value, total


VALUE, TOTAL = count()


def ring(kinds, size):
    place, last, n, held = {}, {}, 0, [None] * size
    for step in STEPS:
        if step[0] in kinds:
            place[step] = n % size
            last[step] = held[n % size]
            held[n % size] = step
            n += 1
    return place, last, held


SCORE_PLACE, SCORE_LAST, SCORE_HELD = ring(("scores", "xscores", "lin_scores"), 2)
BANK_LAST, BANK_HELD = {}, [None] * BANKS
for step in STEPS:
    if step in BANK_OF:
        BANK_LAST[step] = BANK_HELD[BANK_OF[step]]
        BANK_HELD[BANK_OF[step]] = step
UNITS = [x for x in STEPS if x[0] in VALUES_KINDS]
UNIT_AT = {x: n for n, x in enumerate(UNITS)}
HEADS_OUT = [x for x in UNITS if ("heads_out", x) in signals(x)]
HEADS_LAST = {b: a for a, b in zip(HEADS_OUT, HEADS_OUT[1:])}
PRIMED = ("act_freed", "dve_freed", "probs", "masked", "heads_out", "x0", "x1")
SENT = [x for x in STEPS if x[0] in ("k", "kx") or x == ("q", x[1], LIN)]
K_STEPS = [[x for x in STEPS if x[0] in ("k", "kx") and x[1] == s] for s in range(NS)]
K_LAST = {b: a for steps in K_STEPS for a, b in zip(steps, steps[1:])}


def bank_end(s, layer, b):
    return next(x for x in HEADS_OUT if bank_id(x) == (s, layer, b))


def chain_length():
    return sum({"split": 1, "norm": 1, "y": 4 if x[2:] == (FFN0,) else 2}.get(x[0], 0) for x in STEPS)


DVE_CHAIN = chain_length()


def build(nc, x, ctxT, w_lin, w_lin_proj, wx0, wq0, bq0, bk0, bx0_row, w_ffn0, ffn0_row, w_self, wq_self, bq_self,
          bk_self, b_self_row, w_self_out, wx1, wq1, bq1, bk1, bx1_row, w_freq, ffn1_row, const, out):
    with ExitStack() as ctx:
        def sb(name, shape, dt=F32):
            return ctx.enter_context(nc.sbuf_tensor(name, shape, dt))

        def sem(name):
            return ctx.enter_context(nc.semaphore(name))

        C = sb("C", [P, CONST.shape[1]])
        table = {name: C[:, a:b] for name, (a, b) in CONST_AT.items()}
        ident = table["ident"]
        WL = sb("WL", [P, 3 * D])
        WLP = sb("WLP", [P, D])
        WQ = {layer: sb(f"WQ{layer}", [P, G, ROWS]) for layer in (X0, SELF, X1)}
        BQ = {layer: sb(f"BQ{layer}", [ROWS, G]) for layer in (X0, SELF, X1)}
        BK = {layer: sb(f"BK{layer}", [P, 1]) for layer in (X0, SELF, X1)}
        WX = [sb(f"WX{i}", [P, 3, D]) for i in range(2)]
        BXR = [sb(f"BXR{i}", [P, 2, D]) for i in range(2)]
        WS = sb("WS", [P, 2, D])
        BSR = sb("BSR", [P, 2, D])
        WSO = sb("WSO", [P, D])
        WF0 = sb("WF0", [P, D])
        F0R = sb("F0R", [P, 2, D])
        WFR = sb("WFR", [P, 2, D])
        F1R = sb("F1R", [P, D])
        WF1 = sb("WF1", [P, D])
        identr = sb("identr", [P, P], F32R)
        zeros = sb("zeros", [P, T])
        halves = sb("halves", [P, TT])

        def each(name, shape, dt=F32):
            return [sb(f"{name}{s}", shape, dt) for s in range(NS)]

        X = each("X", [P, TT, D])
        XB = each("XB", [P, TT, D])
        XT = each("XT", [P, T])
        CT = each("CT", [P, S])
        SM = each("SM", [P, TT - 1, H * VW])
        QS = each("QS", [P, G, T], F32R)
        KM = each("KM", [P, G, J, T], F32R)
        KT = each("KT", [P, G, J * TAIL], F32R)
        VA = each("VA", [P, TT, H * VW])
        VT = each("VT", [P, G, J * VW])
        OT = each("OT", [P, G // 2, T])
        OC = each("OC", [P, T])
        NEG = each("NEG", [P, G, TT, J])
        NMP = [[sb(f"NMP{s}{i}", [P, TT, P], F32R) for i in range(2)] for s in range(NS)]
        O = each("O", [P, TT, D])
        Z = each("Z", [P, TT, D])
        ST6 = each("ST6", [P, TT, 6])
        MV = each("MV", [P, TT, 2])
        VE = each("VE", [P, TT])
        RST = each("RST", [P, TT])
        REC = each("REC", [P, 2, 2 * H])
        QF = [OC[s][:, :] for s in range(NS)]
        KF = [OT[s][:, 0, :] for s in range(NS)]
        KTOK = [OT[s][:, 1, :].rearrange("p (t d) -> p t d", t=TT) for s in range(NS)]
        T1 = [XB[s][:, :, :].rearrange("p t d -> p (t d)") for s in range(NS)]
        T2 = [SM[s][:, TT - 2, :] for s in range(NS)]
        HI = [SM[s][:, 0, :].bitcast(F32R) for s in range(NS)]
        LO = [SM[s][:, 1, :].bitcast(F32R) for s in range(NS)]
        KHI = [Z[s][:, :, :].rearrange("p t d -> p (t d)").bitcast(F32R) for s in range(NS)]
        KLO = [O[s][:, :, :].rearrange("p t d -> p (t d)").bitcast(F32R) for s in range(NS)]
        KXH = each("KXH", [P, S], F32R)
        KXL = each("KXL", [P, S], F32R)
        SPLITS = {"q": (HI, LO), "k": (KHI, KLO), "kx": (KXH, KXL)}
        MARK = sb("MARK", [P, 1])
        PR = sb("PR", [P, 2, J, T])
        PT = sb("PT", [P, 2, T])
        GT = PT[:, :, 0:D]
        BVM = sb("BVM", [P, 2, D])

        SC = [ctx.enter_context(nc.psum_tensor(f"SC{i}", [P, 2, T], F32)) for i in range(2)]
        BANK = [ctx.enter_context(nc.psum_tensor(f"BANK{i}", [P, T], F32)) for i in range(BANKS)]
        OTP = ctx.enter_context(nc.psum_tensor("OTP", [P, T], F32))

        QD = [nc.dram_tensor(f"QD{s}", (2, P, T), F32, kind="Internal").ap() for s in range(NS)]
        KD = [nc.dram_tensor(f"KD{s}", (2, P, T), F32, kind="Internal").ap() for s in range(NS)]

        sems = {name: sem(name) for name in TOTAL}
        first_weights_in = sem("first_weights_in")
        weights_in = sem("weights_in")
        prep_gpsimd = sem("prep_gpsimd")
        prep_vector = sem("prep_vector")
        prep_tensor = sem("prep_tensor")
        x_in = [sem(f"x_in{s}") for s in range(NS)]
        q_in = [sem(f"q_in{s}") for s in range(NS)]
        q_out = [sem(f"q_out{s}") for s in range(NS)]
        k_out = [sem(f"k_out{s}") for s in range(NS)]
        k_in = [[sem(f"k_in{s}_{j}") for j in range(J)] for s in range(NS)]
        stored = [sem(f"stored{s}") for s in range(NS)]
        dve_self = sem("dve_self")
        aug_in = sem("aug_in")

        def done(eng, it, name, key):
            eng.wait_ge(sems[name], it * TOTAL[name] + VALUE[name, key] + (name in PRIMED))

        def earlier(eng, it, name):
            assert name in PRIMED
            eng.wait_ge(sems[name], it * TOTAL[name] + 1)

        def ready(eng, it, step, *inputs):
            level = {}
            for x in inputs:
                level[freed(x)] = max(level.get(freed(x), 0), VALUE[freed(x), x])
            last = BANK_LAST[step]
            if last is not None:
                level[freed(last)] = max(level.get(freed(last), 0), VALUE[freed(last), last])
            else:
                name = freed(BANK_HELD[BANK_OF[step]])
                level[name] = max(level.get(name, 0), 0)
            for name, value in level.items():
                eng.wait_ge(sems[name], it * TOTAL[name] + value + 1)

        def score_empty(eng, it, step):
            last = SCORE_LAST[step]
            if last is None:
                earlier(eng, it, "probs")
                earlier(eng, it, "masked")
            else:
                done(eng, it, "masked" if last[0] == "lin_scores" else "probs", last)

        def heads_out_free(eng, it, unit):
            end = bank_end(*bank_id(unit))
            if end in HEADS_LAST:
                done(eng, it, "heads_out", HEADS_LAST[end])
            else:
                earlier(eng, it, "heads_out")

        def v_columns(tile, at, n):
            first = tile[:, at:at + 1]
            return bass.AP(tensor=tile.tensor, offset=first.offset,
                           ap=[list(tile.ap[0]), [H // 2 * VW + HALF, 2], [VW, H // 2], [1, n]])

        def x_key(s, layer):
            return ("ln", s, layer - 1)

        def w_k(layer):
            return {LIN: WL[:, D:2 * D], SELF: WS[:, 0, :], X0: WX[0][:, 0, :], X1: WX[1][:, 0, :]}[layer]

        def w_v(layer):
            return {LIN: WL[:, 2 * D:], SELF: WS[:, 1, :], X0: WX[0][:, 1, :], X1: WX[1][:, 1, :]}[layer]

        def w_out(layer):
            return {LIN: WLP[:, :], SELF: WSO[:, :], X0: WX[0][:, 2, :], X1: WX[1][:, 2, :],
                    FFN0: WF0[:, :], FFN1: WF1[:, :]}[layer]

        def v_bias(layer):
            return {SELF: BSR, X0: BXR[0], X1: BXR[1]}[layer][:, 0, :]

        def out_bias(layer):
            return {SELF: BSR[:, 1, :], X0: BXR[0][:, 1, :], X1: BXR[1][:, 1, :], FFN1: F1R[:, :]}[layer]

        def spread(row, n):
            return bass.AP(tensor=row.tensor, offset=row.offset, ap=[list(row.ap[0]), [0, n], list(row.ap[-1])])

        LOADS = {}
        loads_total = {}
        for step in STEPS:
            if step in SENT:
                name = ("q" if step[0] == "q" else "k", step[1])
                loads_total[name] = loads_total.get(name, 0) + 1
                LOADS[step] = loads_total[name]

        def landed(eng, it, step, planes=range(J)):
            name = ("q" if step[0] == "q" else "k", step[1])
            s = step[1]
            for arrived in [q_in[s]] if step[0] == "q" else [k_in[s][j] for j in planes]:
                eng.wait_ge(arrived, (it * loads_total[name] + LOADS[step]) * 16 * 3)

        N_FIRST = 7
        NW = 16
        N_GPREP = 2 + 2 * NS + 1 + 1
        N_VZERO = 1 + 2 * NS
        N_VPREP = N_VZERO + 5 + 2 + J * (1 + 3 * NS)

        def prepared(eng):
            eng.wait_ge(weights_in, 16 * NW)
            eng.wait_ge(prep_gpsimd, N_GPREP)
            eng.wait_ge(prep_vector, N_VPREP)
            eng.wait_ge(aug_in, 16 * NS * G)

        block = ctx.enter_context(nc.Block())

        @block.sync
        def _(sp):
            row = lambda r: bass.AP(tensor=r.tensor, offset=r.offset, ap=[[0, P]] + [list(a) for a in r.ap])
            for dst, src in ((C[:, :], const), (WL[:, :], w_lin), (WF0[:, :], w_ffn0), (F0R[:, :, :], row(ffn0_row)),
                             (WFR[:, :, :], w_freq), (BXR[0][:, :, :], row(bx0_row)), (BXR[1][:, :, :], row(bx1_row))):
                sp.dma_start(dst, src).then_inc(first_weights_in, 16)
            for dst, src in ((WLP[:, :], w_lin_proj), (WX[0][:, :, :], wx0), (WX[1][:, :, :], wx1),
                             (WQ[X0][:, :, :], wq0), (WQ[SELF][:, :, :], wq_self), (WQ[X1][:, :, :], wq1),
                             (BQ[X0][:, :], bq0), (BQ[SELF][:, :], bq_self), (BQ[X1][:, :], bq1),
                             (BK[X0][:, :], bk0), (BK[SELF][:, :], bk_self), (BK[X1][:, :], bk1),
                             (WS[:, :, :], w_self), (BSR[:, :, :], row(b_self_row)), (WSO[:, :], w_self_out),
                             (F1R[:, :], row(ffn1_row))):
                sp.dma_start(dst, src).then_inc(weights_in, 16)
            sp.wait_ge(prep_vector, N_VPREP)
            for s in range(NS):
                for g in range(G):
                    sp.dma_start(KM[s][ROWS:P, g, :, :].bitcast(F32), PR[ROWS:P, 0, :, :]).then_inc(aug_in, 16)
            sp.wait_ge(prep_gpsimd, N_GPREP)
            with sp.Fori(0, PAIRS) as it:
                for step in STEPS:
                    kind, s = step[0], step[1]
                    if step in SENT:
                        done(sp, it, "lo" if step[2] == LIN else "dve_freed", step)
                        n = S if kind == "kx" else T
                        hi, lo = [part[s] for part in SPLITS[kind]]
                        name, out_sem, in_sem, dram = ("q", q_out[s], q_in[s], QD[s]) if kind == "q" else \
                                                      ("k", k_out[s], k_in[s], KD[s])
                        sp.dma_start(dram[0, :, 0:n], hi[:, 0:n].bitcast(F32)).then_inc(out_sem, 16)
                        sp.dma_start(dram[1, :, 0:n], lo[:, 0:n].bitcast(F32)).then_inc(out_sem, 16)
                        sp.wait_ge(out_sem, (it * loads_total[name, s] + LOADS[step]) * 32)
                        if kind == "q":
                            for blk, part in enumerate((0, 0, 1)):
                                r = slice(SPLIT * blk, SPLIT * blk + SPLIT)
                                sp.dma_start(QS[s][r, :, :].bitcast(F32),
                                             dram[part].rearrange("(g r) t -> r g t", g=G)).then_inc(in_sem, 16)
                            continue
                        for j in range(J):
                            for blk, part in enumerate((0, 1, 0)):
                                r = SPLIT * blk + DH * j
                                src = dram[part].rearrange("(g j d) t -> j d g t", g=G, j=J)[j, :, :, 0:n]
                                sp.dma_start(KM[s][r:r + DH, :, j, 0:n].bitcast(F32), src).then_inc(in_sem[j], 16)

        @block.gpsimd
        def _(pool):
            for ap, v in [(zeros[:, :], 0.0), (VT[0][:, :, :], 0.0), (VT[1][:, :, :], 0.0), (halves[:, :], -0.5),
                          (VA[0][:, :, :], 0.0), (VA[1][:, :, :], 0.0), (KM[0][0:ROWS, :, :, :].bitcast(F32), 0.0)]:
                nc.gpsimd.memset(ap, v).then_inc(prep_gpsimd, 1)
            pool.wait_ge(prep_gpsimd, N_GPREP - 2)
            last = None
            for s in range(NS):
                for tt in range(TT):
                    last = nc.gpsimd.memset(v_columns(VA[s][:, tt, :], DH, 1), 1.0)
            last.then_inc(prep_gpsimd, 1)
            with pool.Fori(0, PAIRS) as it:
                for step in STEPS:
                    kind, s = step[0], step[1]
                    if kind == "kx":
                        landed(pool, it, step)
                        nc.gpsimd.tensor_tensor(KT[s][0:ROWS, :, :].rearrange("p g (j n) -> p (g j) n", j=J),
                                                KM[s][0:ROWS, :, :, TAIL_AT:S].rearrange("p g j n -> p (g j) n")
                                                .bitcast(F32),
                                                zeros[0:ROWS, :].rearrange("p (a n) -> p a n", n=TAIL), ALU.add)\
                          .then_inc(sems["tail"], 1)
                    if kind == "y":
                        done(pool, it, f"var{s}", step)
                        nc.gpsimd.tensor_tensor(RST[s][:, :], VE[s][:, :], halves[:, :], ALU.pow)\
                          .then_inc(sems[f"rstd{s}"], 1)
                    if kind == "ln":
                        layer = step[2]
                        if layer in BIAS_AFTER:
                            done(pool, it, f"x{s}", step)
                            nc.gpsimd.tensor_tensor(XB[s][:, :, :], X[s][:, :, :],
                                                    spread(out_bias(BIAS_AFTER[layer]), TT), ALU.add)\
                              .then_inc(sems[f"xb{s}"], 1)

        @block.scalar
        def _(act):
            for name in ("act_freed", "probs", "heads_out"):
                act.sem_inc(sems[name], 1)
            for s in range(NS):
                act.sem_inc(stored[s], 1)
            with act.Fori(0, PAIRS) as it:
                for step in STEPS:
                    kind, s = step[0], step[1]
                    bank = BANK[BANK_OF[step]] if step in BANK_OF else None
                    if kind == "load":
                        earlier(act, it, f"x{s}")
                        act.wait_ge(stored[s], it * 16 + 1)
                        act.dma_start(X[s][:, :, :], x[bass.ds(it * NS + s, 1), :, :].rearrange(
                            "b (t p) d -> p (b t) d", p=P)).then_inc(x_in[s], 16)
                        act.dma_start(CT[s][:, :], ctxT[bass.ds(it * NS + s, 1), :, :].rearrange(
                            "b p n -> p (b n)")).then_inc(x_in[s], 16)
                    if kind == "store":
                        done(act, it, f"x{s}", ("ln", s, FFN1))
                        act.dma_start(out[bass.ds(it * NS + s, 1), :, :].rearrange("b (t p) d -> p (b t) d", p=P),
                                     X[s][:, :, :]).then_inc(stored[s], 16)
                    if kind == "xt":
                        done(act, it, "bank_full", step)
                        nc.scalar.activation(XT[s][:, :], bank[:, :], ACT.Copy).then_inc(sems["act_freed"], 1)
                    if kind == "turn":
                        done(act, it, "bank_full", step)
                        nc.scalar.activation(OC[s][:, :], bank[:, :], ACT.Copy).then_inc(sems["act_freed"], 1)
                    if kind in ("q", "k", "ktok") and step[2] == LIN:
                        done(act, it, "clipped", step)
                        nc.scalar.activation(T2[s], T1[s], ACT.Exp).then_inc(sems["exped"], 1)
                        if kind != "ktok":
                            done(act, it, "dve_freed", step)
                            nc.scalar.activation((HI if kind == "q" else KHI)[s][:, :],
                                                 (QF if kind == "q" else KF)[s], ACT.Copy)\
                              .then_inc(sems["hi"], 1)
                    elif kind == "q":
                        done(act, it, "bank_full", step)
                        g = step[3]
                        nc.scalar.activation(QS[s][0:ROWS, g, :], bank[0:ROWS, :], ACT.Identity,
                                             bias=BQ[step[2]][:, g:g + 1]).then_inc(sems["hi"], 1)
                    elif kind in ("k", "kx"):
                        n = S if kind == "kx" else T
                        done(act, it, "bank_full", step)
                        if step in K_LAST:
                            landed(act, it, K_LAST[step])
                        nc.scalar.activation(SPLITS[kind][0][s][:, 0:n], bank[:, 0:n], ACT.Identity,
                                             bias=BK[step[2]][:, :]).then_inc(sems["hi"], 1)
                    if kind == "shift":
                        done(act, it, "bank_full", step)
                        nc.scalar.activation(QS[s][ROWS:P, step[3], :], bank[ROWS:P, :], ACT.Copy)\
                          .then_inc(sems["act_freed"], 1)
                    if kind == "scores":
                        _, _, layer, g, kt, half = step
                        place = SCORE_PLACE[step]
                        unit = UNIT_AT[("values", s, layer, g, kt)]
                        done(act, it, "scores_full", step)
                        if unit >= 2:
                            done(act, it, "values_done", UNITS[unit - 2])
                        nc.scalar.activation(PR[:, unit % 2, 2 * half:2 * half + 2, :], SC[place][:, :, :], ACT.Exp,
                                             scale=SCALE).then_inc(sems["probs"], 1)
                    if kind == "xscores":
                        _, _, layer, g, part = step
                        place = SCORE_PLACE[step]
                        unit = UNIT_AT[("xvalues", s, layer, g)]
                        done(act, it, "scores_full", step)
                        if unit >= 2:
                            done(act, it, "values_done", UNITS[unit - 2])
                        if part < 2:
                            nc.scalar.activation(PR[:, unit % 2, 2 * part:2 * part + 2, :], SC[place][:, :, :],
                                                 ACT.Exp, scale=SCALE).then_inc(sems["probs"], 1)
                        else:
                            nc.scalar.activation(PT[:, unit % 2, :], SC[place][:, 0, :], ACT.Exp,
                                                 scale=SCALE).then_inc(sems["probs"], 1)
                    if ("heads_out", step) in signals(step):
                        done(act, it, "values_done", step)
                        if step[2] == LIN:
                            nc.scalar.activation(OT[s][:, step[3] % 2, :], OTP[:, :], ACT.Identity, bias=table["eps"])\
                              .then_inc(sems["heads_out"], 1)
                        else:
                            nc.scalar.activation(OT[s][:, step[3] % 2, :], OTP[:, :], ACT.Copy)\
                              .then_inc(sems["heads_out"], 1)
            for s in range(NS):
                act.wait_ge(stored[s], PAIRS * 16 + 1)

        @block.vector
        def _(dve):
            for name in ("dve_freed", "masked", "x0", "x1"):
                dve.sem_inc(sems[name], 1)
            for ap in (KM[1][0:ROWS, :, :, :], *[NMP[s][i][:, :, :] for s in range(NS) for i in range(2)]):
                nc.vector.memset(ap.bitcast(F32), 0.0).then_inc(prep_vector, 1)
            dve.wait_ge(first_weights_in, 16 * N_FIRST)
            nc.vector.tensor_scalar(GT[:, 0, :], WF0[:, :], 0.0, 2.0, ALU.is_ge, ALU.mult).then_inc(prep_vector, 1)
            dve.wait_ge(prep_vector, N_VZERO + 1)
            nc.vector.scalar_tensor_tensor(WF0[:, :], GT[:, 0, :], -1.0, F0R[:, 0, :], ALU.add, ALU.mult)\
              .then_inc(prep_vector, 1)
            dve.wait_ge(prep_vector, N_VZERO + 2)
            dve.wait_ge(prep_tensor, 1)
            nc.vector.tensor_copy(GT[:, :, :], BANK[0][:, 0:2 * D].rearrange("p (a d) -> p a d", a=2))\
              .then_inc(prep_vector, 1)
            dve.wait_ge(prep_tensor, 2)
            nc.vector.tensor_scalar(WF1[:, :], BANK[0][:, 0:D], 1.0 / D, None, ALU.mult).then_inc(prep_vector, 1)
            nc.vector.tensor_copy(identr[:, :], ident).then_inc(prep_vector, 1)
            for i in range(2):
                nc.vector.tensor_scalar(BVM[:, i, :], BXR[i][:, 0, :], table["tailmask"], None, ALU.mult)\
                  .then_inc(prep_vector, 1)
            dve.wait_ge(prep_gpsimd, 1 + NS)
            for j in range(J):
                aug = table["augmask"][ROWS:P, j:j + 1]
                nc.vector.tensor_scalar(PR[ROWS:P, 0, j, :], zeros[ROWS:P, :], aug, None, ALU.add)\
                  .then_inc(prep_vector, 1)
                for s in range(NS):
                    nc.vector.tensor_scalar(KT[s][ROWS:P, :, j * TAIL:j * TAIL + TAIL],
                                            zeros[ROWS:P, 0:G * TAIL].rearrange("p (g n) -> p g n", g=G), aug, None,
                                            ALU.add).then_inc(prep_vector, 1)
                    r = slice(VW * j, VW * j + VW)
                    for up in range(2):
                        nc.vector.tensor_scalar(
                            VT[s][r, up * G // 2:(up + 1) * G // 2, VW * j + up * HALF + DH], zeros[r, 0:G // 2],
                            table["tailmask"][r, :], None, ALU.add).then_inc(prep_vector, 1)
            with dve.Fori(0, PAIRS) as it:
                chain = [0]
                CH = DVE_CHAIN

                def link(ins):
                    chain[0] += 1
                    ins.then_inc(dve_self, 1)
                    dve.wait_ge(dve_self, it * CH + chain[0])

                for step in STEPS:
                    kind, s = step[0], step[1]
                    bank = BANK[BANK_OF[step]] if step in BANK_OF else None
                    if kind in ("q", "k", "ktok") and step[2] == LIN:
                        done(dve, it, "bank_full", step)
                        nc.vector.tensor_scalar(T1[s], bank[:, :], 0.0, None, ALU.min).then_inc(sems["clipped"], 1)
                        done(dve, it, "exped", step)
                        dst = {"q": QF[s], "k": KF[s], "ktok": OT[s][:, 1, :]}[kind]
                        nc.vector.scalar_tensor_tensor(dst, bank[:, :], 0.0, T2[s], ALU.max, ALU.add)\
                          .then_inc(sems["dve_freed"], 1)
                        if kind != "ktok":
                            done(dve, it, "hi", step)
                            done(dve, it, "dve_freed", step)
                            nc.vector.tensor_tensor((LO if kind == "q" else KLO)[s][:, :], dst,
                                                    (HI if kind == "q" else KHI)[s][:, :].bitcast(F32), ALU.subtract)\
                              .then_inc(sems["lo"], 1)
                    elif kind == "q":
                        g = step[3]
                        low = slice(2 * SPLIT, ROWS)
                        done(dve, it, "hi", step)
                        nc.vector.scalar_tensor_tensor(QS[s][low, g, :], bank[low, :], BQ[step[2]][low, g:g + 1],
                                                       QS[s][low, g, :].bitcast(F32), ALU.add, ALU.subtract)\
                          .then_inc(sems["dve_freed"], 1)
                    elif kind in ("k", "kx"):
                        n = S if kind == "kx" else T
                        hi, lo = [part[s] for part in SPLITS[kind]]
                        done(dve, it, "hi", step)
                        nc.vector.scalar_tensor_tensor(lo[:, 0:n], bank[:, 0:n], BK[step[2]][:, :],
                                                       hi[:, 0:n].bitcast(F32), ALU.add, ALU.subtract)\
                          .then_inc(sems["dve_freed"], 1)
                    if kind == "v":
                        if step[2] == LIN:
                            prepared(dve)
                        done(dve, it, "bank_full", step)
                        for tt in range(TT):
                            dst = v_columns(VA[s][:, tt, :], 0, DH)
                            src = bank[:, tt * D:tt * D + D].rearrange("p (u h c) -> p u h c", u=2, c=DH)
                            if step[2] == LIN:
                                ins = nc.vector.tensor_copy(dst, src)
                            else:
                                vb = v_bias(step[2]).rearrange("p (u h c) -> p u h c", u=2, c=DH)
                                ins = nc.vector.tensor_tensor(dst, src, vb, ALU.add)
                        ins.then_inc(sems["dve_freed"], 1)
                    if kind == "vx":
                        i = 0 if step[2] == X0 else 1
                        done(dve, it, "bank_full", step)
                        vb = v_bias(step[2]).rearrange("p (u h c) -> p u h c", u=2, c=DH)
                        nc.vector.tensor_tensor(v_columns(VA[s][:, 0, :], 0, DH),
                                                bank[:, 0:D].rearrange("p (u h c) -> p u h c", u=2, c=DH), vb,
                                                ALU.add)
                        tail = bank[:, D:2 * D].rearrange("p (g j c) -> p g j c", g=G, j=J)
                        vb = BVM[:, i, :].rearrange("p (g j c) -> p g j c", g=G, j=J)
                        for j in range(J):
                            r = slice(VW * j, VW * j + VW)
                            for up in range(2):
                                g = slice(up * G // 2, (up + 1) * G // 2)
                                c = VW * j + up * HALF
                                ins = nc.vector.scalar_tensor_tensor(VT[s][r, g, c:c + DH], tail[r, g, j, :],
                                                                     table["tailmask"][r, :], vb[r, g, j, :],
                                                                     ALU.mult, ALU.add)
                        ins.then_inc(sems["dve_freed"], 1)
                    if kind == "state":
                        done(dve, it, "bank_full", step)
                        if step[3] == 0:
                            landed(dve, it, ("q", s, LIN))
                        nc.vector.tensor_tensor(SM[s][:, step[3], :], bank[:, :], table["blockdiag"], ALU.mult)\
                          .then_inc(sems["dve_freed"], 1)
                    if kind == "lin_scores":
                        _, _, layer, g, p = step
                        place = SCORE_PLACE[step]
                        unit = UNIT_AT[("lin_values", s, layer, g, p)]
                        done(dve, it, "scores_full", step)
                        if unit >= 2:
                            done(dve, it, "values_done", UNITS[unit - 2])
                        for c in range(2):
                            ins = nc.vector.tensor_tensor(
                                PR[:, unit % 2, c, :].rearrange("p (j t) -> p j t", j=J),
                                SC[place][:, c, :].rearrange("p (j t) -> p j t", j=J),
                                spread(table["causal"], J), ALU.mult)
                        ins.then_inc(sems["masked"], 1)
                    if kind == "max":
                        _, _, layer, g, qt, j = step
                        done(dve, it, "bank_full", step)
                        if layer == SELF:
                            src, dst = bank[:, :], NEG[s][:, g, qt, j:j + 1]
                        else:
                            src = bank[:, 0:2 * S].rearrange("p (a n) -> p a n", a=2)
                            dst = NEG[s][:, g, qt, 2 * j:2 * j + 2]
                        nc.vector.tensor_reduce(dst, src, AX.X, ALU.max, negate=True).then_inc(sems["dve_freed"], 1)
                    if kind == "split":
                        _, _, layer, g = step
                        place = GROUPS.index(g)
                        done(dve, it, "dve_freed", [x for x in STEPS if x[0:4] == ("max", s, layer, g)][-1])
                        if place >= 2:
                            done(dve, it, "act_freed", ("shift", s, layer, GROUPS[place - 2]))
                        nmp = NMP[s][place % 2]
                        hi = nmp[:, :, ROWS:ROWS + J]
                        link(nc.vector.tensor_copy(hi, NEG[s][:, g, :, :]))
                        nc.vector.tensor_tensor(nmp[:, :, ROWS + J:ROWS + 2 * J], NEG[s][:, g, :, :],
                                                hi.bitcast(F32), ALU.subtract).then_inc(sems["shift_split"], 1)
                    if kind == "norm":
                        b = step[3]
                        done(dve, it, "bank_full", step)
                        m = bank[:, :].rearrange("p (t j u c) -> p t j u c", t=TT, j=J, u=2)
                        den = bank[:, :].rearrange("p (n c) -> p n c", c=HALF)[:, :, DH]
                        link(nc.vector.reciprocal(REC[s][:, b, :], den))
                        o = O[s][:, :, :].rearrange("p t (u b j c) -> p t u b j c", u=2, b=2, j=J)
                        for u in range(2):
                            r = REC[s][:, b, u:u + 1]
                            rb = bass.AP(tensor=r.tensor, offset=r.offset,
                                         ap=[list(r.ap[0]), [2 * J, TT], [2, J], [0, DH]])
                            ins = nc.vector.tensor_tensor(o[:, :, u, b, :, :], m[:, :, :, u, 0:DH], rb, ALU.mult)
                        ins.then_inc(sems["dve_freed"], 1)
                    if kind == "y":
                        layer = step[2]
                        z = Z[s][:, :, :]
                        y = bank[:, :].rearrange("p (t d) -> p t d", t=TT)
                        done(dve, it, "bank_full", step)
                        if layer == FFN0:
                            for tt in range(TT):
                                ins = nc.vector.tensor_tensor(Z[s][:, tt, :], y[:, tt, :], F0R[:, 1, :], ALU.add)
                            ins.then_inc(sems["dve_freed"], 1)
                            done(dve, it, "dve_freed", step)
                            link(nc.vector.tensor_scalar(z, z, MAX_VAL, -MAX_VAL, ALU.min, ALU.max))
                            link(nc.vector.tensor_tensor(z, z, X[s][:, :, :], ALU.add))
                        else:
                            res = X[s] if layer == LIN else XB[s]
                            if layer != LIN:
                                done(dve, it, f"xb{s}", ("ln", s, layer - 1))
                            nc.vector.tensor_tensor(z, y, res[:, :, :], ALU.add).then_inc(sems["dve_freed"], 1)
                            done(dve, it, "dve_freed", step)
                        for tt in range(TT):
                            ins = nc.vector.bn_stats(ST6[s][:, tt, :], Z[s][:, tt, :])
                        link(ins)
                        nc.vector.memset(MARK[:, :], 0.0)
                        for tt in range(TT):
                            ins = nc.vector.bn_aggr(MV[s][:, tt, :], ST6[s][:, tt, :])
                        link(ins)
                        nc.vector.tensor_scalar(VE[s][:, :], MV[s][:, :, 1], EPS_LN, None, ALU.add)\
                          .then_inc(sems[f"var{s}"], 1)
                    if kind == "ln":
                        done(dve, it, f"rstd{s}", ("y", s, step[2]))
                        for tt in range(TT):
                            ins = nc.vector.tensor_scalar(X[s][:, tt, :], Z[s][:, tt, :], MV[s][:, tt, 0:1],
                                                          RST[s][:, tt:tt + 1], ALU.subtract, ALU.mult)
                        ins.then_inc(sems[f"x{s}"], 1)
                assert chain[0] == CH, chain[0]

        @block.tensor
        def _(pe):
            mm = nc.tensor.matmul
            pe.wait_ge(first_weights_in, 16 * N_FIRST)
            mm(BANK[0][:, 0:D], WFR[:, 0, :], table["cos"], start=True, stop=False)
            mm(BANK[0][:, 0:D], WFR[:, 1, :], table["sin"], start=False, stop=True)
            mm(BANK[0][:, D:2 * D], WFR[:, 1, :], table["cos"], start=True, stop=False)
            mm(BANK[0][:, D:2 * D], WFR[:, 0, :], table["nsin"], start=False, stop=True).then_inc(prep_tensor, 1)
            pe.wait_ge(prep_vector, N_VZERO + 3)
            mm(BANK[0][:, 0:D], GT[:, 0, :], table["cos"], start=True, stop=False)
            mm(BANK[0][:, 0:D], GT[:, 1, :], table["nsin"], start=False, stop=True).then_inc(prep_tensor, 1)
            pe.wait_ge(prep_vector, N_VZERO + 4)
            with pe.Fori(0, PAIRS) as it:
                for step in STEPS:
                    kind, s = step[0], step[1]
                    bank = BANK[BANK_OF[step]] if step in BANK_OF else None
                    if kind == "xt":
                        if step[2] == LIN:
                            pe.wait_ge(x_in[s], it * 32 + 32)
                        else:
                            done(pe, it, f"x{s}", x_key(s, step[2]))
                        ready(pe, it, step)
                        for tt in range(TT):
                            ins = nc.tensor.transpose(bank[:, tt * P:tt * P + P], X[s][:, tt, :], ident)
                        ins.then_inc(sems["bank_full"], 1)
                    if kind in ("q", "k"):
                        ready(pe, it, step, ("xt", s, step[2]))
                        if kind == "q" and step[2] != LIN:
                            rows, w = slice(0, ROWS), WQ[step[2]][:, step[3], :]
                        else:
                            rows, w = slice(0, P), WL[:, 0:D] if kind == "q" else w_k(step[2])
                        mm(bank[rows, :], w, XT[s][:, :], start=True, stop=True).then_inc(sems["bank_full"], 1)
                    if kind == "kx":
                        ready(pe, it, step)
                        pe.wait_ge(x_in[s], it * 32 + 32)
                        mm(bank[:, 0:S], w_k(step[2]), CT[s][:, :], start=True, stop=True)\
                            .then_inc(sems["bank_full"], 1)
                    if kind == "vx":
                        ready(pe, it, step)
                        mm(bank[:, 0:D], CT[s][:, 0:P], w_v(step[2]), start=True, stop=True)
                        for j in range(J):
                            ins = mm(bank[VW * j:VW * j + VW, D:2 * D], CT[s][:, TAIL_AT:S], w_v(step[2]),
                                     start=True, stop=True)
                        ins.then_inc(sems["bank_full"], 1)
                    if kind in ("v", "ktok"):
                        ready(pe, it, step, ("xt", s, step[2]))
                        w = w_v(step[2]) if kind == "v" else w_k(step[2])
                        for tt in range(TT):
                            ins = mm(bank[:, tt * D:tt * D + D], XT[s][:, tt * P:tt * P + P], w, start=True, stop=True)
                        ins.then_inc(sems["bank_full"], 1)
                    if kind == "state":
                        c = step[3]
                        if c == 0:
                            prepared(pe)
                        ready(pe, it, step, ("v", s, LIN), ("ktok", s, LIN))
                        mm(bank[:, :], KTOK[s][:, c, :], VA[s][:, c, :], start=(c == 0), stop=True,
                           skip_group_check=True).then_inc(sems["bank_full"], 1)
                    if kind == "lin_scores":
                        _, _, layer, g, p = step
                        if p == 0:
                            if g == 0:
                                landed(pe, it, ("q", s, layer))
                                landed(pe, it, ("k", s, layer))
                        score_empty(pe, it, step)
                        place = SCORE_PLACE[step]
                        for c in range(2):
                            t = slice((2 * p + c) * P, (2 * p + c + 1) * P)
                            for j in range(J):
                                ins = mm(SC[place][:, c, j * P:j * P + P], KM[s][0:ROWS, g, j, t], QS[s][0:ROWS, g, t],
                                         start=True, stop=True)
                        ins.then_inc(sems["scores_full"], 1)
                    if kind == "lin_values":
                        _, _, layer, g, p = step
                        unit = UNIT_AT[step]
                        done(pe, it, "masked", ("lin_scores", s, layer, g, p))
                        if p == 0:
                            if g < G // 2:
                                heads_out_free(pe, it, step)
                            if g == 0:
                                done(pe, it, "dve_freed", ("state", s, layer, TT - 2))
                        for c in range(2):
                            n = 2 * p + c
                            t = slice(n * P, n * P + P)
                            if n:
                                mm(OTP[:, t], SM[s][:, n - 1, g * P:g * P + P], QF[s][:, t], start=False,
                                   stop=False, skip_group_check=True)
                            for j in range(J):
                                h = g * J + j
                                ins = mm(OTP[VW * j:VW * j + VW, t], VA[s][:, n, h * VW:h * VW + VW],
                                         PR[:, unit % 2, c, j * P:j * P + P], start=(n == 0 and g < G // 2), stop=True,
                                         skip_group_check=True)
                        ins.then_inc(sems["values_done"], 1)
                    if kind == "max":
                        _, _, layer, g, qt, j = step
                        if qt == 0 and g == GROUPS[0]:
                            if layer == SELF:
                                landed(pe, it, ("k", s, layer), [j])
                            elif j == 0:
                                landed(pe, it, ("kx", s, layer))
                        ready(pe, it, step, ("q", s, layer, g))
                        q = QS[s][0:ROWS, g, qt * P:qt * P + P]
                        if layer == SELF:
                            ins = mm(bank[:, :], q, KM[s][0:ROWS, g, j, :], start=True, stop=True)
                        else:
                            ins = mm(bank[:, 0:2 * S].rearrange("p (a n) -> p a n", a=2), q,
                                     KM[s][0:ROWS, g, 2 * j:2 * j + 2, 0:S], start=True, stop=True)
                        ins.then_inc(sems["bank_full"], 1)
                    if kind == "shift":
                        done(pe, it, "shift_split", ("split", *step[1:]))
                        ready(pe, it, step)
                        for qt in range(TT):
                            ins = mm(bank[:, qt * P:qt * P + P], NMP[s][GROUPS.index(step[3]) % 2][:, qt, :],
                                     identr[:, :], start=True, stop=True)
                        ins.then_inc(sems["bank_full"], 1)
                    if kind == "scores":
                        _, _, layer, g, kt, half = step
                        if kt == 0 and half == 0:
                            done(pe, it, "act_freed", ("shift", s, layer, g))
                        score_empty(pe, it, step)
                        place = SCORE_PLACE[step]
                        for a in range(2):
                            ins = mm(SC[place][:, a, :], KM[s][:, g, 2 * half + a, kt * P:kt * P + P], QS[s][:, g, :],
                                     start=True, stop=True)
                        ins.then_inc(sems["scores_full"], 1)
                    if kind == "values":
                        _, _, layer, g, kt = step
                        unit = UNIT_AT[step]
                        done(pe, it, "probs", ("scores", s, layer, g, kt, 1))
                        if kt == 0:
                            if g < G // 2:
                                heads_out_free(pe, it, step)
                            if g == 0:
                                done(pe, it, "dve_freed", ("v", s, layer))
                        for j in range(J):
                            h = g * J + j
                            ins = mm(OTP[VW * j:VW * j + VW, :], VA[s][:, kt, h * VW:h * VW + VW],
                                     PR[:, unit % 2, j, :], start=(kt == 0 and g < G // 2),
                                     stop=(kt == TT - 1 and g >= G // 2))
                        ins.then_inc(sems["values_done"], 1)
                    if kind == "xscores":
                        _, _, layer, g, part = step
                        if part == 0:
                            done(pe, it, "act_freed", ("shift", s, layer, g))
                            if g == 0:
                                done(pe, it, "tail", ("kx", s, layer))
                        score_empty(pe, it, step)
                        place = SCORE_PLACE[step]
                        if part < 2:
                            for a in range(2):
                                ins = mm(SC[place][:, a, :], KM[s][:, g, 2 * part + a, 0:P], QS[s][:, g, :],
                                         start=True, stop=True)
                        else:
                            ins = mm(SC[place][:, 0, :], KT[s][:, g, :], QS[s][:, g, :], start=True, stop=True)
                        ins.then_inc(sems["scores_full"], 1)
                    if kind == "xvalues":
                        _, _, layer, g = step
                        unit = UNIT_AT[step]
                        done(pe, it, "probs", ("xscores", s, layer, g, 2))
                        if g < G // 2:
                            heads_out_free(pe, it, step)
                        if g == 0:
                            done(pe, it, "dve_freed", ("vx", s, layer))
                        mm(OTP[:, :], VT[s][:, g, :], PT[:, unit % 2, :], start=(g < G // 2), stop=False,
                           skip_group_check=True)
                        for j in range(J):
                            h = g * J + j
                            ins = mm(OTP[VW * j:VW * j + VW, :], VA[s][:, 0, h * VW:h * VW + VW], PR[:, unit % 2, j, :],
                                     start=False, stop=True, skip_group_check=True)
                        ins.then_inc(sems["values_done"], 1)
                    if kind == "norm":
                        _, _, layer, b = step
                        ready(pe, it, step)
                        done(pe, it, "heads_out", bank_end(s, layer, b))
                        for tt in range(TT):
                            ins = nc.tensor.transpose(bank[:, tt * P:tt * P + P], OT[s][:, b, tt * P:tt * P + P], ident)
                        ins.then_inc(sems["bank_full"], 1)
                    if kind == "turn":
                        ready(pe, it, step, *[("norm", s, step[2], b) for b in range(G // 2)])
                        for tt in range(TT):
                            ins = nc.tensor.transpose(bank[:, tt * P:tt * P + P], O[s][:, tt, :], ident)
                        ins.then_inc(sems["bank_full"], 1)
                    if kind == "y":
                        layer = step[2]
                        ready(pe, it, step, ("xt" if layer in (FFN0, FFN1) else "turn", s, layer))
                        src = XT[s] if layer in (FFN0, FFN1) else OC[s]
                        for tt in range(TT):
                            ins = mm(bank[:, tt * D:tt * D + D], src[:, tt * P:tt * P + P], w_out(layer),
                                     start=True, stop=True)
                        ins.then_inc(sems["bank_full"], 1)


def kernel(**inputs):
    import numpy as _np
    import concourse.bacc as _bacc
    from concourse import mybir as _mybir
    from concourse.bass_utils import run_bass_kernel_spmd as _run

    a = {k: _np.asarray(v) for k, v in inputs.items()}
    cross = lambda pre, k, v, o: _np.stack([a[pre + n].T for n in (k, v, o)], axis=1)

    def thrice(w):
        return _np.tile(w.reshape(*w.shape[:-1], G, SPLIT), ROWS // SPLIT)

    arrays = {
        "x": a["x"],
        "ctxT": a["ctx_1024"].transpose(0, 2, 1),
        "w_lin": a["L0_attn_w_attn"],
        "w_lin_proj": a["L0_attn_w_proj"],
        "wx0": cross("L0_xattn_W", "k", "v", "o"),
        "wq0": thrice(a["L0_xattn_Wq"].T),
        "bq0": thrice(a["L0_xattn_bq"]).T,
        "bk0": a["L0_xattn_bk"].reshape(D, 1),
        "bx0_row": _np.stack([a["L0_xattn_bv"], a["L0_xattn_bo"]]),
        "w_ffn0": a["L0_ffn_weights"].T,
        "ffn0_row": _np.stack([a["L0_ffn_scale"], a["L0_ffn_bias"]]),
        "w_self": a["L1_attn_w_qkv"][:, D:].reshape(D, 2, D),
        "wq_self": thrice(a["L1_attn_w_qkv"][:, 0:D]),
        "bq_self": thrice(a["L1_attn_b_qkv"][0:D]).T,
        "bk_self": a["L1_attn_b_qkv"][D:2 * D].reshape(D, 1),
        "b_self_row": _np.stack([a["L1_attn_b_qkv"][2 * D:], a["L1_attn_b_out"]]),
        "w_self_out": a["L1_attn_w_out"],
        "wx1": cross("L1_xattn_w_", "k", "v", "o"),
        "wq1": thrice(a["L1_xattn_w_q"].T),
        "bq1": thrice(a["L1_xattn_b_q"]).T,
        "bk1": a["L1_xattn_b_k"].reshape(D, 1),
        "bx1_row": _np.stack([a["L1_xattn_b_v"], a["L1_xattn_b_o"]]),
        "w_freq": _np.stack([a["L1_ffn_w_freq_real"], a["L1_ffn_w_freq_imag"]], axis=1),
        "ffn1_row": a["L1_ffn_bias"],
        "const": CONST,
    }
    arrays = {f"in_{k}_dram": _np.ascontiguousarray(v) for k, v in arrays.items()}
    nc = _bacc.Bacc("TRN2", target_bir_lowering=False, num_devices=1)
    args = [nc.dram_tensor(k, v.shape, _mybir.dt.from_np(v.dtype), kind="ExternalInput").ap()
            for k, v in arrays.items()]
    args.append(nc.dram_tensor("out_0_dram", (B, T, D), _mybir.dt.from_np(_np.dtype("float32")),
                               kind="ExternalOutput").ap())
    build(nc, *args)
    r = _run(nc, [arrays], core_ids=[0])
    return r.results[0]["out_0_dram"]
```
